# Optimizing a Trainium2 kernel written in Bass

```python
import numpy as np
import jax
import jax.numpy as jnp

def _softmax(x, axis=-1):
    return jax.nn.softmax(x, axis=axis)

def _gelu(x):
    return jax.nn.gelu(x, approximate=True)

def _silu(x):
    return jax.nn.silu(x)

def _sigmoid(x):
    return jax.nn.sigmoid(x)

def _layernorm(x, axis=-1, eps=1e-05):
    m = jnp.mean(x, axis=axis, keepdims=True)
    v = jnp.var(x, axis=axis, keepdims=True)
    return (x - m) / jnp.sqrt(v + eps)

def _scatter_add(tgt, idx, src, axis=0):
    return tgt.at[idx].add(src)

def _segment_sum(src, seg, n):
    return jax.ops.segment_sum(src, seg, n)
kernel_name = 'mk_macaron_d1_jaxref_r8_404431'

def setup_inputs(seed: int=0):
    np.random.seed(seed)
    _w = jnp.asarray

    def _L0_attn_setup():
        import jax, jax.numpy as jnp
        import numpy as np
        B, S, H = (2, 256, 256)
        NH = 16
        Q_LORA, KV_LORA = (192, 64)
        D_K, D_R, D_V = (128, 64, 128)
        IH, ID, TOPK = (8, 128, 8)

        def _rope_tables(dim, end, base=10000.0):
            inv = 1.0 / base ** (np.arange(0, dim, 2)[:dim // 2].astype(np.float32) / dim)
            freqs = np.outer(np.arange(end, dtype=np.float32), inv)
            return (jnp.asarray(np.cos(freqs)), jnp.asarray(np.sin(freqs)))

        def _apply_rope(x, cos, sin):
            xr, xi = (x[..., 0::2], x[..., 1::2])
            c, s_ = (cos[None, None], sin[None, None])
            out_r = xr * c - xi * s_
            out_i = xr * s_ + xi * c
            return jnp.stack([out_r, out_i], axis=-1).reshape(x.shape)
        key = jax.random.key(seed)
        ks = jax.random.split(key, 16)
        std = 0.02

        def w(k, shape):
            return jax.random.normal(k, shape, dtype=jnp.float32) * std
        return {'x': jax.random.normal(ks[0], (B, S, H), dtype=jnp.float32), 'W_c': w(ks[1], (H, KV_LORA)), 'W_cp': w(ks[2], (H, Q_LORA)), 'W_qc': w(ks[3], (Q_LORA, NH * D_K)), 'W_qr': w(ks[4], (Q_LORA, NH * D_R)), 'W_kc': w(ks[5], (KV_LORA, NH * D_K)), 'W_kr': w(ks[6], (H, D_R)), 'W_v': w(ks[7], (KV_LORA, NH * D_V)), 'W_o': w(ks[8], (NH * D_V, H)), 'W_idx': w(ks[9], (H, IH * ID)), 'W_gate': w(ks[10], (H, IH)), 'W_sq': w(ks[11], (ID, ID)), 'W_sk': w(ks[12], (ID, ID)), 'W_sv': w(ks[13], (ID, ID)), 'W_iout': w(ks[14], (ID, H))}
    _L0_attn_in = _L0_attn_setup()

    def _L0_ffn_setup():
        import jax, jax.numpy as jnp
        import numpy as np
        NUM_EXPERTS_PER_TOK = 2
        key = jax.random.key(seed)
        k1, k2, k3, k4 = jax.random.split(key, 4)
        B, S, D, O, E = (4, 256, 256, 256, 8)
        x = jax.random.normal(k1, (B, S, D), dtype=jnp.float32)
        gate_w = jax.random.normal(k2, (E, D), dtype=jnp.float32) * (1.0 / np.sqrt(D))
        expert_w = jax.random.normal(k3, (E, O, D), dtype=jnp.float32) * (1.0 / np.sqrt(D))
        expert_b = jax.random.normal(k4, (E, O), dtype=jnp.float32) * 0.01
        return {'x': x, 'gate_w': gate_w, 'expert_w': expert_w, 'expert_b': expert_b}
    _L0_ffn_in = _L0_ffn_setup()
    _d = {'L0_attn_x': _L0_attn_in['x'], 'L0_attn_W_c': _L0_attn_in['W_c'], 'L0_attn_W_cp': _L0_attn_in['W_cp'], 'L0_attn_W_qc': _L0_attn_in['W_qc'], 'L0_attn_W_qr': _L0_attn_in['W_qr'], 'L0_attn_W_kc': _L0_attn_in['W_kc'], 'L0_attn_W_kr': _L0_attn_in['W_kr'], 'L0_attn_W_v': _L0_attn_in['W_v'], 'L0_attn_W_o': _L0_attn_in['W_o'], 'L0_attn_W_idx': _L0_attn_in['W_idx'], 'L0_attn_W_gate': _L0_attn_in['W_gate'], 'L0_attn_W_sq': _L0_attn_in['W_sq'], 'L0_attn_W_sk': _L0_attn_in['W_sk'], 'L0_attn_W_sv': _L0_attn_in['W_sv'], 'L0_attn_W_iout': _L0_attn_in['W_iout'], 'L0_ffn_gate_w': _L0_ffn_in['gate_w'], 'L0_ffn_expert_w': _L0_ffn_in['expert_w'], 'L0_ffn_expert_b': _L0_ffn_in['expert_b']}
    _x0 = _d['L0_attn_x']
    _d['L0_attn_x'] = jax.random.normal(jax.random.fold_in(jax.random.key(seed), 1), (1, 1024, 256), dtype=_x0.dtype)
    del _x0
    return _d

def reference(L0_attn_x, L0_attn_W_c, L0_attn_W_cp, L0_attn_W_qc, L0_attn_W_qr, L0_attn_W_kc, L0_attn_W_kr, L0_attn_W_v, L0_attn_W_o, L0_attn_W_idx, L0_attn_W_gate, L0_attn_W_sq, L0_attn_W_sk, L0_attn_W_sv, L0_attn_W_iout, L0_ffn_gate_w, L0_ffn_expert_w, L0_ffn_expert_b):

    def _L0_attn_ref(x, W_c, W_cp, W_qc, W_qr, W_kc, W_kr, W_v, W_o, W_idx, W_gate, W_sq, W_sk, W_sv, W_iout):
        import jax, jax.numpy as jnp
        import numpy as np
        B, S, H = (2, 256, 256)
        NH = 16
        Q_LORA, KV_LORA = (192, 64)
        D_K, D_R, D_V = (128, 64, 128)
        IH, ID, TOPK = (8, 128, 8)

        def _rope_tables(dim, end, base=10000.0):
            inv = 1.0 / base ** (np.arange(0, dim, 2)[:dim // 2].astype(np.float32) / dim)
            freqs = np.outer(np.arange(end, dtype=np.float32), inv)
            return (jnp.asarray(np.cos(freqs)), jnp.asarray(np.sin(freqs)))

        def _apply_rope(x, cos, sin):
            xr, xi = (x[..., 0::2], x[..., 1::2])
            c, s_ = (cos[None, None], sin[None, None])
            out_r = xr * c - xi * s_
            out_i = xr * s_ + xi * c
            return jnp.stack([out_r, out_i], axis=-1).reshape(x.shape)
        b, s, _ = x.shape
        cos, sin = _rope_tables(D_R, s)
        c = x @ W_c
        cp = x @ W_cp
        q_c = (cp @ W_qc).reshape(b, s, NH, D_K).transpose(0, 2, 1, 3)
        k_c = (c @ W_kc).reshape(b, s, NH, D_K).transpose(0, 2, 1, 3)
        q_r = (cp @ W_qr).reshape(b, s, NH, D_R).transpose(0, 2, 1, 3)
        k_r = jnp.broadcast_to((x @ W_kr)[:, None], (b, NH, s, D_R))
        v = (c @ W_v).reshape(b, s, NH, D_V).transpose(0, 2, 1, 3)
        q_r = _apply_rope(q_r, cos, sin)
        k_r = _apply_rope(k_r, cos, sin)
        q = jnp.concatenate([q_c, q_r], axis=-1)
        k = jnp.concatenate([k_c, k_r], axis=-1)
        scale = 1.0 / np.sqrt(D_K + D_R)
        scores = jnp.einsum('bhqd,bhkd->bhqk', q, k) * scale
        causal = jnp.triu(jnp.ones((s, s), dtype=bool), 1)
        scores = jnp.where(causal[None, None], -jnp.inf, scores)
        probs = jax.nn.softmax(scores.astype(jnp.float32), axis=-1).astype(q.dtype)
        attn = jnp.einsum('bhqk,bhkd->bhqd', probs, v)
        idx_states = (x @ W_idx).reshape(b, s, IH, ID)
        gate = x @ W_gate
        _, top_idx = jax.lax.top_k(gate.transpose(0, 2, 1), TOPK)
        ish = idx_states.transpose(0, 2, 1, 3)
        sel = jnp.take_along_axis(ish, top_idx[..., None], axis=2)
        sq, sk, sv = (sel @ W_sq, sel @ W_sk, sel @ W_sv)
        sprobs = jax.nn.softmax(jnp.einsum('bhqd,bhkd->bhqk', sq, sk) / np.sqrt(ID), axis=-1)
        sout = jnp.einsum('bhqk,bhkd->bhqd', sprobs, sv)
        sparse_out = sout.reshape(b, IH * TOPK, ID) @ W_iout
        io = sparse_out.reshape(b, IH, TOPK, H).mean(axis=2)
        io = jnp.broadcast_to(io[:, :, None, :D_V], (b, IH, s, D_V))
        io = jnp.repeat(io, NH // IH, axis=1)
        attn = attn + io
        out = attn.transpose(0, 2, 1, 3).reshape(b, s, NH * D_V) @ W_o
        return out

    def _L0_ffn_ref(x, gate_w, expert_w, expert_b):
        import jax, jax.numpy as jnp
        import numpy as np
        NUM_EXPERTS_PER_TOK = 2
        B, S, D = x.shape
        xf = x.reshape(B * S, D)
        gate_logits = xf @ gate_w.T
        top_vals, top_idx = jax.lax.top_k(gate_logits, NUM_EXPERTS_PER_TOK)
        w = jax.nn.softmax(top_vals.astype(jnp.float32), axis=-1).astype(x.dtype)
        y_all = jnp.einsum('td,eod->teo', xf, expert_w) + expert_b[None, :, :]
        y_sel = jnp.take_along_axis(y_all, top_idx[:, :, None], axis=1)
        out = jnp.sum(y_sel * w[:, :, None], axis=1)
        return out.reshape(B, S, -1)
    x = L0_attn_x
    x = x + 0.5 * _L0_ffn_ref(_layernorm(x, axis=-1), L0_ffn_gate_w, L0_ffn_expert_w, L0_ffn_expert_b)
    x = x + _L0_attn_ref(_layernorm(x, axis=-1), L0_attn_W_c, L0_attn_W_cp, L0_attn_W_qc, L0_attn_W_qr, L0_attn_W_kc, L0_attn_W_kr, L0_attn_W_v, L0_attn_W_o, L0_attn_W_idx, L0_attn_W_gate, L0_attn_W_sq, L0_attn_W_sk, L0_attn_W_sv, L0_attn_W_iout)
    x = x + 0.5 * _L0_ffn_ref(_layernorm(x, axis=-1), L0_ffn_gate_w, L0_ffn_expert_w, L0_ffn_expert_b)
    return x

_drawn_inputs = setup_inputs


def setup_inputs(seed=0):
    import zlib

    import numpy as np

    out = dict(_drawn_inputs(seed))
    spreads = {}
    factors = {'L0_attn_W_c': 8.0,
     'L0_attn_W_cp': 8.0,
     'L0_attn_W_qc': 8.0,
     'L0_attn_W_qr': 8.0,
     'L0_attn_W_kc': 8.0,
     'L0_attn_W_kr': 8.0,
     'L0_attn_W_v': 6.204,
     'L0_attn_W_o': 3.022,
     'L0_attn_W_idx': 3.884,
     'L0_attn_W_gate': 2.936,
     'L0_attn_W_sq': 8.0,
     'L0_attn_W_sk': 8.0,
     'L0_attn_W_sv': 3.552,
     'L0_attn_W_iout': 3.281,
     'L0_ffn_expert_b': 5.42}
    for name, (base, spread) in spreads.items():
        noise = np.random.default_rng([zlib.crc32(name.encode()), seed]).standard_normal(out[name].shape)
        drawn = base * np.exp(spread * noise) if base else spread * noise
        out[name] = jnp.asarray(drawn.astype(out[name].dtype))
    for name, factor in factors.items():
        out[name] = (out[name] * factor).astype(out[name].dtype)
    return out
```

```python
import numpy as np
import concourse.bass as bass
from concourse import mybir
from contextlib import ExitStack

F32 = mybir.dt.float32
BF16 = mybir.dt.bfloat16
U32 = mybir.dt.uint32
ALU = mybir.AluOpType
ACT = mybir.ActivationFunctionType
AX = mybir.AxisListType

P = 128
T, D = 1024, 256
NT, KD = T // P, D // P
E, O = 8, 256
CHUNKS = E // 2
NH, DK, DR, DV = 16, 128, 64, 128
KV, QL = 64, 192
QK = QL // 2
PAIRS = NH // 2
IH, ID, TOPK = 8, 128, 8
SEL = IH * TOPK
GT = 4
SCALE = 1.0 / float(np.sqrt(DK + DR))
EPS = 1e-5
MASKED = -1e30
BANK = 512


class Ring:

    def __init__(self, banks, full, free, order):
        self.banks, self.full, self.free = banks, full, free
        self.at = {key: i for i, key in enumerate(order)}
        self.n = len(order)

    def use(self, key):
        i = self.at[key]
        b = i % len(self.banks)
        return self.banks[b], self.full[b], self.free[b], i // len(self.banks)


Y_ORDER = [("y", 0, t, c) for t in range(NT) for c in range(CHUNKS)] \
    + [("absorb_k", i) for i in range(4)] + [("absorb_v", i) for i in range(4)] \
    + [("index_gate", i) for i in range(2)] + [("latent_kv", i) for i in range(2)] \
    + [("latent_q", i) for i in range(4)]
Y_TAIL = [("project", t) for t in range(NT)] \
    + [("y", 1, t, c) for t in range(NT) for c in range(CHUNKS)]
T_ORDER = [("xnT", 0, i) for i in range(4)] + [("wT", 0, i) for i in range(2)] \
    + [("xnT", 1, i) for i in range(4)] + [("keysT", i) for i in range(2)] \
    + [("queryT", j) for j in range(NT - 1)]
M_ORDER = [("gate", 0)] + [("io_row",), ("io_all",)] + [("query", j) for j in range(NT)]
C_ORDER = [("bias", 0, i) for i in range(4)] \
    + [(s,) for s in ("onehot", "rows", "selected", "sqkv", "sscores", "smean", "sout", "io")]

UNITS = 2 * NT
LAG = 2
R_AT = {1: 3, 0: 12}
PV_AT = {1: 3, 0: 12}


def tiles_of(v):
    return v // 2 + 1


def chunks_of(v):
    return (tiles_of(v) + GT - 1) // GT


def loop_items():
    items = []
    for u in range(UNITS):
        v = (u - LAG) % UNITS
        items += [(u, "probsT", (v, c), u < LAG) for c in range(chunks_of(v))]
        if u % 2 == 1:
            j = (u // 2 - 1) % NT
            items.append((u, "queryT", (j,), False))
        for group, at in R_AT.items():
            if at == u:
                items.append((u, "sumsT", (group,), group == 1))
    return items


LOOP_ITEMS = loop_items()
assert len(LOOP_ITEMS) % 2 == 0


def turn_items(g, pair_count=PAIRS):
    first, last = isinstance(g, int) and g == 0, isinstance(g, int) and g == pair_count - 1
    base = len(T_ORDER)
    before = [len([i for i in range(base) if i % 2 == b]) for b in range(2)]
    missing = [len([1 for n, it in enumerate(LOOP_ITEMS) if it[3] and (base + n) % 2 == b]) for b in range(2)]
    count, out = [0, 0], {u: [] for u in range(UNITS)}
    for n, (u, kind, args, needs_earlier) in enumerate(LOOP_ITEMS):
        if first and needs_earlier:
            continue
        if last and kind == "queryT" and args[0] != NT - 1:
            continue
        b = (base + n) % 2
        start = before[b] if first else before[b] - missing[b] + g * (len(LOOP_ITEMS) // 2)
        out[u].append((kind, args, b, start + count[b]))
        count[b] += 1
    return out


def turn_tail():
    last = turn_items(PAIRS - 1)
    seen = [0, 0]
    for items in last.values():
        for _, _, b, prior in items:
            seen[b] = prior + 1
    order = [("probsT", v, c) for v in (UNITS - 2, UNITS - 1) for c in range(chunks_of(v))] \
        + [("sumsT", 1)] + [("xnT", 2, i) for i in range(4)] + [("wT", 1, i) for i in range(2)]
    out = {}
    for i, key in enumerate(order):
        out[key] = (i % 2, seen[i % 2])
        seen[i % 2] += 1
    return out


def build(nc, a, out):
    ctx = ExitStack()
    with ctx:
        def sb(name, shape, dt=F32):
            return ctx.enter_context(nc.sbuf_tensor(name, shape, dt))

        def sem(name):
            return ctx.enter_context(nc.semaphore(name))

        x = sb("x", [P, NT, D])
        wexp = sb("wexp", [P, CHUNKS, KD, 2 * O])
        wgate = sb("wgate", [P, KD, E])
        bexp = sb("bexp", [E, O])
        wts = sb("wts", [P, NT, E])
        wT = sb("wT", [E, T])
        stats = sb("stats", [P, NT, 6])
        mv = sb("mv", [P, NT, 2])
        varE = sb("varE", [P, NT])
        sd = sb("sd", [P, NT])
        rs0 = sb("rs0", [P, NT])
        rstd = sb("rstd", [P, NT])
        logits = sb("logits", [P, NT, E])
        top = sb("top", [P, NT, 8])
        topi = sb("topi", [P, NT, 8], U32)
        topf = sb("topf", [P, NT, 2])
        gap = sb("gap", [P, NT])
        egap = sb("egap", [P, NT])
        w1 = sb("w1", [P, NT])
        w2 = sb("w2", [P, NT])
        hot = sb("hot", [P, 2, NT, E])
        iota8 = sb("iota8", [P, NT, E])

        wq = sb("wq", [QK, 2, NH, P])
        wcp = sb("wcp", [P, KD, QL])
        wkv = sb("wkv", [P, KD, P])
        widx_gate = sb("widx_gate", [P, KD, IH])
        cpT = sb("cpT", [QK, 2, T])
        kf = sb("kf", [P, NT, P])
        keysT = sb("keysT", [P, T])
        qtok = sb("qtok", [P, 2, 2, P])
        ropeA = sb("ropeA", [P, 4, DR])
        ropeB = sb("ropeB", [P, 4, DR])
        cosT = sb("cosT", [P, NT, DR])
        sinT = sb("sinT", [P, NT, DR])
        qT = sb("qT", [P, 2, T])
        probs = sb("probs", [P, 4, T])
        xn = probs[:, 0:2, :].rearrange("p a (t n) -> p (a t) n", n=D)
        xnT = probs[:, 2:4, :]
        pT0 = sb("pT0", [P, 2, GT, BANK])
        pT1 = sb("pT1", [P, 2, NT, BANK])
        ctxT = sb("ctxT", [P, PAIRS, T])
        absV = sb("absV", [P, PAIRS, O])
        negmax = sb("negmax", [P, 4])
        sums = sb("sums", [P, 2, GT, 2])
        rsum = sb("rsum", [P, 2, GT, 2])
        rwide = sb("rwide", [P, GT, 2, 64])
        rT = sb("rT", [P, 2, BANK])
        ident = sb("ident", [P, P])
        identb = sb("identb", [P, P], BF16)
        causal = sb("causal", [P, P], BF16)
        ones = sb("ones", [P, P])
        iorow = sb("iorow", [1, O])

        early1 = pT1[:, :, :, :].rearrange("p h k n -> p (h k n)")
        wo = early1[:, 0:4096].rearrange("p (h n) -> p h n", h=NH)
        wvT = early1[:, 4096:5120].rearrange("p (h n) -> p h n", h=NH)
        wkcT = early1[:, 5120:6144].rearrange("p (h n) -> p h n", h=NH)
        wosum = early1[:, 6144:8192].rearrange("p (h n) -> p h n", h=IH)
        early0 = pT0[:, :, :, :].rearrange("p h k n -> p (h k n)")
        wqcT = early0[:, 0:3072].rearrange("p (h n) -> p h n", h=NH)
        ws3 = early0[:, 3072:3584].rearrange("p (w n) -> p w n", w=4)
        early2 = ctxT[:, :, :].rearrange("p g n -> p (g n)")
        widx = early2[:, 0:2048].rearrange("p (k n) -> p k n", k=KD)
        iotaT = early2[0:SEL, 2048:3072]
        hotT = early2[0:SEL, 3072:4096]
        onehot = early2[:, 4096:4608].rearrange("p (t s) -> p t s", t=NT)
        gT = early2[0:IH, 4608:5632]
        rowsT = early2[:, 5632:5760].rearrange("p (k s) -> p k s", k=KD)
        selT = early2[:, 5760:5824]
        sqkT = early2[:, 5824:5952].rearrange("p (w s) -> p w s", w=2)
        sv = early2[0:SEL, 5952:6080]
        blockmask = early2[0:SEL, 6080:6144]
        groups = early2[0:SEL, 6144:6152]
        ssc = early2[0:SEL, 6152:6216]
        sp_ = early2[0:SEL, 6216:6280]
        smean = early2[0:SEL, 6280:6288]
        soutT = early2[:, 6288:6296]
        ioT = early2[:, 6296:6304]
        gtop = early2[0:IH, 6304:6312]
        gidx = early2[0:IH, 6312:6320].bitcast(U32)
        gidf = early2[0:IH, 6320:6328]
        idxp = early2[0:SEL, 6328:6329]
        snm = early2[0:SEL, 6329:6330]
        ssum = early2[0:SEL, 6330:6331]
        srs = early2[0:SEL, 6331:6332]
        sprob = early2[0:SEL, 6336:6400]

        S = [ctx.enter_context(nc.psum_tensor(f"S{i}", [P, 2 * BANK], F32)) for i in range(2)]
        TB = [ctx.enter_context(nc.psum_tensor(f"TB{i}", [P, BANK], F32)) for i in range(2)]
        M = ctx.enter_context(nc.psum_tensor("M", [P, BANK], F32))
        C = ctx.enter_context(nc.psum_tensor("C", [P, BANK], F32))
        YB = [S[i // 2][:, (i % 2) * BANK:(i % 2 + 1) * BANK] for i in range(4)]

        x_in = [sem(f"x_in{i}") for i in range(4)]
        wexp_in = [sem(f"wexp_in{i}") for i in range(CHUNKS)]
        gate_in, latent_in, absorb_in, rope_in = sem("gate_in"), sem("latent_in"), sem("absorb_in"), sem("rope_in")
        wo_in, index_in = sem("wo_in"), sem("index_in")
        ident_made, masks_made, iotas_made = sem("ident_made"), sem("masks_made"), sem("iotas_made")
        pool_step = sem("pool_step")
        dve_step = sem("dve_step")
        var_ready, sd_ready, xn_ready = sem("var_ready"), sem("sd_ready"), sem("xn_ready")
        gap_ready, egap_ready, wts_ready = sem("gap_ready"), sem("egap_ready"), sem("wts_ready")
        y_full, y_free = [sem(f"y_full{i}") for i in range(4)], [sem(f"y_free{i}") for i in range(4)]
        t_full, t_free = [sem(f"t_full{i}") for i in range(2)], [sem(f"t_free{i}") for i in range(2)]
        m_full, m_free, c_full, c_free = sem("m_full"), sem("m_free"), sem("c_full"), sem("c_free")
        index_listed, index_spread, hot_ready = sem("index_listed"), sem("index_spread"), sem("hot_ready")
        sscore_ready, sexp_ready, sprob_ready = sem("sscore_ready"), sem("sexp_ready"), sem("sprob_ready")
        wosum_ready = sem("wosum_ready")
        key_roped = sem("key_roped")
        query_roped = sem("query_roped")
        scores_ready, negmax_ready, probs_ready = sem("scores_ready"), sem("negmax_ready"), sem("probs_ready")
        rsum_ready, rwide_ready = sem("rsum_ready"), sem("rwide_ready")
        out_done = sem("out_done")

        yr = Ring(YB, y_full, y_free, Y_ORDER)
        tr = Ring([TB[0], TB[1]], t_full, t_free, T_ORDER)
        mr = Ring([M], [m_full], [m_free], M_ORDER)
        cr = Ring([C], [c_full], [c_free], C_ORDER)
        y_base = len(Y_ORDER) // 4
        tail = turn_tail()

        def y_use(key):
            if key in yr.at:
                return yr.use(key)
            i = Y_TAIL.index(key)
            return YB[i % 4], y_full[i % 4], y_free[i % 4], y_base + i // 4

        def t_use(key):
            if key in tr.at:
                return tr.use(key)
            b, prior = tail[key]
            return TB[b], t_full[b], t_free[b], prior

        def m_use(key):
            if key in mr.at:
                return mr.use(key)
            assert key == ("gate", 1)
            return M, m_full, m_free, mr.n + (PAIRS - 1) * NT

        def c_use(key):
            if key in cr.at:
                return cr.use(key)
            return C, c_full, c_free, cr.n + 2 * PAIRS + key[2]

        def m_query(g, j):
            return mr.n + g * NT + j

        def c_group(g, group):
            return cr.n + 2 * g + group

        def probsT_drain(drain, use, v, c):
            qt, h = v // 2, v % 2
            n = min(GT, tiles_of(v) - GT * c)
            pT = pT0 if qt < GT else pT1
            drain(use, pT[:, h, GT * c:GT * c + n, P * (qt % GT):P * (qt % GT + 1)],
                  lambda b: b[:, 0:n * P].rearrange("p (k n) -> p k n", k=n))

        block = ctx.enter_context(nc.Block())

        @block.sync
        def _(sp):
            x_v = a["x"].rearrange("(t p) n -> p t n", p=P)
            for i in range(4):
                sp.dma_start(x[:, 2 * i:2 * i + 2, :], x_v[:, 2 * i:2 * i + 2, :]).then_inc(x_in[i], 16)
            sp.dma_start(wgate[:, :, :], a["gate_w"]).then_inc(gate_in, 16)
            sp.dma_start(bexp[:, :], a["expert_b"]).then_inc(gate_in, 16)
            for c in range(CHUNKS):
                sp.dma_start(wexp[:, c, :, :], a["expert_w"][:, c, :, :]).then_inc(wexp_in[c], 16)
            sp.dma_start(wqcT, a["W_qc"]).then_inc(absorb_in, 16)
            sp.dma_start(wkcT, a["W_kc"]).then_inc(absorb_in, 16)
            sp.dma_start(wvT, a["W_v"]).then_inc(wo_in, 16)
            sp.dma_start(wo, a["W_o"]).then_inc(wo_in, 16)
            sp.dma_start(wq[:, :, :, KV:P], a["W_qr"]).then_inc(latent_in, 16)
            sp.dma_start(wcp[:, :, :], a["W_cp"]).then_inc(latent_in, 16)
            sp.dma_start(wkv[:, :, 0:KV], a["W_c"]).then_inc(latent_in, 16)
            sp.dma_start(wkv[:, :, KV:P], a["W_kr"]).then_inc(latent_in, 16)
            sp.dma_start(cosT[:, :, :], a["cos"]).then_inc(rope_in, 16)
            sp.dma_start(sinT[:, :, :], a["sin"]).then_inc(rope_in, 16)
            sp.dma_start(widx, a["W_idx"]).then_inc(index_in, 16)
            sp.dma_start(widx_gate[:, :, :], a["W_gate"]).then_inc(index_in, 16)
            for n, name in enumerate(("W_sq", "W_sk", "W_sv", "W_iout")):
                sp.dma_start(ws3[:, n, :], a[name]).then_inc(index_in, 16)
            sp.wait_ge(index_listed, 1)
            sp.dma_start(idxp, gidf).then_inc(index_spread, 16)
            out_v = out.rearrange("(t p) n -> p t n", p=P)
            for i in range(4):
                use = c_use(("bias", 1, i))
                sp.wait_ge(use[2], use[3] + 1)
                sp.dma_start(out_v[:, 2 * i:2 * i + 2, :], x[:, 2 * i:2 * i + 2, :]).then_inc(out_done, 16)
            sp.wait_ge(out_done, 16 * 4)

        @block.gpsimd
        def _(pool):
            steps = [0]

            def settle(ins):
                ins.then_inc(pool_step, 1)
                steps[0] += 1
                pool.wait_ge(pool_step, steps[0])

            settle(pool.memset(ident[:, :], 0.0))
            pool.affine_select(out=ident[:, :], in_=ident[:, :], compare_op=ALU.not_equal, fill=1.0, base=0,
                               pattern=[[-1, P]], channel_multiplier=1).then_inc(ident_made, 1)
            pool.iota(iota8[:, :, :], [[0, NT], [1, E]], base=0, channel_multiplier=0,
                      allow_small_or_imprecise_dtypes=True).then_inc(iotas_made, 1)
            pool.wait_ge(ident_made, 1)
            pool.tensor_copy(identb[:, :], ident[:, :]).then_inc(masks_made, 1)
            settle(pool.memset(causal[:, :], 0.0))
            pool.affine_select(out=causal[:, :], in_=causal[:, :], compare_op=ALU.is_ge, fill=MASKED, base=0,
                               pattern=[[-1, P]], channel_multiplier=1).then_inc(masks_made, 1)
            pool.memset(ones[:, :], 1.0).then_inc(masks_made, 1)
            pool.iota(iotaT, [[1, T]], base=0, channel_multiplier=0,
                      allow_small_or_imprecise_dtypes=True).then_inc(iotas_made, 1)
            settle(pool.memset(blockmask, 0.0))
            bm = blockmask.rearrange("p (h j) -> p h j", h=IH)
            settle(pool.affine_select(out=bm, in_=bm, compare_op=ALU.is_ge, fill=MASKED, base=0,
                                      pattern=[[-TOPK, IH], [0, TOPK]], channel_multiplier=1))
            pool.affine_select(out=bm, in_=bm, compare_op=ALU.is_ge, fill=MASKED, base=TOPK - 1,
                               pattern=[[TOPK, IH], [0, TOPK]], channel_multiplier=-1).then_inc(masks_made, 1)
            settle(pool.memset(groups, 1.0 / TOPK))
            settle(pool.affine_select(out=groups, in_=groups, compare_op=ALU.is_ge, fill=0.0, base=0,
                                      pattern=[[-TOPK, IH]], channel_multiplier=1))
            pool.affine_select(out=groups, in_=groups, compare_op=ALU.is_ge, fill=0.0, base=TOPK - 1,
                               pattern=[[TOPK, IH]], channel_multiplier=-1).then_inc(masks_made, 1)
            pool.wait_ge(wo_in, 32)
            wo_p = wo.rearrange("p (i two) n -> p i two n", two=2)
            pool.tensor_tensor(wosum, wo_p[:, :, 0, :], wo_p[:, :, 1, :], ALU.add).then_inc(wosum_ready, 1)

            def rope(view, cos, sin, n, done):
                h = DR // 2
                pool.tensor_tensor(ropeA[:, 0:n, :], view, cos, ALU.mult).then_inc(pool_step, 1)
                pool.tensor_tensor(ropeB[:, 0:n, 0:h], view[:, :, h:DR], sin[:, :, 0:h], ALU.mult).then_inc(pool_step, 1)
                pool.tensor_tensor(ropeB[:, 0:n, h:DR], view[:, :, 0:h], sin[:, :, h:DR], ALU.mult).then_inc(pool_step, 1)

            def rope_add(view, n, done):
                pool.tensor_tensor(view, ropeA[:, 0:n, :], ropeB[:, 0:n, :], ALU.add).then_inc(done, 1)

            pool.wait_ge(rope_in, 32)
            for i in range(2):
                view = kf[:, 4 * i:4 * i + 4, KV:P]
                use = yr.use(("latent_kv", i))
                pool.wait_ge(use[2], use[3] + 1)
                if i:
                    pool.wait_ge(key_roped, i)
                rope(view, cosT[:, 4 * i:4 * i + 4, :], sinT[:, 4 * i:4 * i + 4, :], 4, key_roped)
                steps[0] += 3
                pool.wait_ge(pool_step, steps[0])
                rope_add(view, 4, key_roped)
            pool.wait_ge(key_roped, 2)
            step_base = steps[0]

            def query_rope(n, j):
                view = qtok[:, j % 2, :, KV:P]
                tab = [t[:, j, :].unsqueeze(1).to_broadcast([P, 2, DR]) for t in (cosT, sinT)]
                pool.wait_ge(m_free, mr.at[("query", 0)] + 1 + n)
                if not isinstance(n, int) or n > 0:
                    pool.wait_ge(query_roped, n)
                rope(view, tab[0], tab[1], 2, query_roped)
                pool.wait_ge(pool_step, step_base + 3 + 3 * n)
                rope_add(view, 2, query_roped)

            def spread(n, group):
                pool.wait_ge(rsum_ready, n + 1)
                wide = rsum[:, group, :, :].unsqueeze(3).to_broadcast([P, GT, 2, 64])
                one = ones[:, 0:1].unsqueeze(2).unsqueeze(3).to_broadcast([P, GT, 2, 64])
                pool.tensor_tensor(rwide[:, :, :, :], wide, one, ALU.mult).then_inc(rwide_ready, 1)

            for j in range(NT):
                query_rope(j, j)

            def body(g):
                last = isinstance(g, int) and g == PAIRS - 1
                first = isinstance(g, int) and g == 0
                for u in range(UNITS):
                    if u == 1 and not first:
                        spread(2 * g - 1, 1)
                    if u == 9:
                        spread(2 * g, 0)
                    if u % 2 == 0 and not last:
                        query_rope(NT + g * NT + u // 2, u // 2)

            body(0)
            with pool.Fori(1, PAIRS - 1) as g:
                body(g)
            body(PAIRS - 1)
            spread(2 * PAIRS - 1, 1)

        @block.scalar
        def _(act):
            def root(n, half):
                act.wait_ge(var_ready, 2 * n + half + 1)
                act.activation(sd[:, 4 * half:4 * half + 4], varE[:, 4 * half:4 * half + 4], ACT.Sqrt) \
                    .then_inc(sd_ready, 1)

            def drain(use, dst, src_of, scale=None):
                bank, full, free, prior = use
                act.wait_ge(full, prior + 1)
                if scale is None:
                    act.copy(dst, src_of(bank)).then_inc(free, 1)
                else:
                    act.activation(dst, src_of(bank), ACT.Copy, scale=scale).then_inc(free, 1)

            def xnT_drain(n, i):
                drain(t_use(("xnT", n, i)), xnT[:, :, 256 * i:256 * i + 256],
                      lambda b: b[:, :].rearrange("p (k n) -> p k n", k=KD))

            def ffn(f):
                act.wait_ge(gap_ready, f + 1)
                act.activation(egap[:, :], gap[:, :], ACT.Exp).then_inc(egap_ready, 1)
                for i in range(2):
                    drain(t_use(("wT", f, i)), wT[:, BANK * i:BANK * (i + 1)], lambda b: b[0:E, :])

            root(0, 0)
            root(0, 1)
            for i in range(4):
                xnT_drain(0, i)
            ffn(0)
            root(1, 0)
            for i in range(4):
                k, half = i // 2, i % 2
                drain(yr.use(("absorb_k", i)), wq[:, k, 8 * half:8 * half + 8, 0:KV],
                      lambda b: b[0:QK, :].rearrange("p (h n) -> p h n", h=8))
            for i in range(4):
                drain(yr.use(("absorb_v", i)), absV[:, 2 * i:2 * i + 2, :],
                      lambda b: b[:, :].rearrange("p (h n) -> p h n", h=2))
            root(1, 1)
            for i in range(4):
                xnT_drain(1, i)
            for i in range(2):
                drain(yr.use(("index_gate", i)), gT[:, BANK * i:BANK * (i + 1)], lambda b: b[0:IH, :])
            for i in range(2):
                drain(yr.use(("latent_kv", i)), kf[:, 4 * i:4 * i + 4, :],
                      lambda b: b[:, :].rearrange("p (t n) -> p t n", t=4))
            for i in range(4):
                m, n = i // 2, i % 2
                drain(yr.use(("latent_q", i)), cpT[:, m, BANK * n:BANK * (n + 1)], lambda b: b[0:QK, :])
            for i in range(2):
                drain(tr.use(("keysT", i)), keysT[:, BANK * i:BANK * (i + 1)], lambda b: b[:, :])

            def query_copy(prior, j):
                act.wait_ge(m_full, prior + 1)
                act.copy(qtok[:, j % 2, :, :], M[:, 0:2 * P].rearrange("p (h n) -> p h n", h=2)).then_inc(m_free, 1)

            def queryT_drain(use, j):
                drain(use, qT[:, :, P * j:P * (j + 1)],
                      lambda b: b[:, 0:2 * P].rearrange("p (h n) -> p h n", h=2), scale=SCALE)

            act.wait_ge(sscore_ready, 1)
            act.activation(sp_, ssc, ACT.Exp, bias=snm, accum_out=ssum).then_inc(sexp_ready, 1)
            for j in range(NT):
                query_copy(mr.use(("query", j))[3], j)
                if j:
                    queryT_drain(tr.use(("queryT", j - 1)), j - 1)

            def body(g):
                last = isinstance(g, int) and g == PAIRS - 1
                items = turn_items(g)
                for u in range(UNITS):
                    qt, h = u // 2, u % 2
                    for kind, args, b, prior in items[u]:
                        use = (TB[b], t_full[b], t_free[b], prior)
                        if kind == "probsT" and args[1] == 1:
                            probsT_drain(drain, use, *args)
                        elif kind == "queryT":
                            queryT_drain(use, args[0])
                        elif kind == "sumsT":
                            drain(use, rT[:, args[0], :], lambda bank: bank[:, :])
                    act.wait_ge(negmax_ready, UNITS * g + u + 1)
                    act.activation(probs[:, u % 4, 0:P * (qt + 1)], S[u % 2][:, 0:P * (qt + 1)], ACT.Exp,
                                   bias=negmax[:, u % 4:u % 4 + 1],
                                   accum_out=sums[:, qt // GT, qt % GT, h:h + 1]).then_inc(probs_ready, 1)
                    if h == 0 and not last:
                        query_copy(m_query(g, qt), qt)

            body(0)
            with act.Fori(1, PAIRS - 1) as g:
                body(g)
            body(PAIRS - 1)
            for v in (UNITS - 2, UNITS - 1):
                probsT_drain(drain, t_use(("probsT", v, 1)), v, 1)
            drain(t_use(("sumsT", 1)), rT[:, 1, :], lambda bank: bank[:, :])
            root(2, 0)
            root(2, 1)
            for i in range(4):
                xnT_drain(2, i)
            ffn(1)

        @block.tensor
        def _(pe):
            def begin(use):
                bank, full, free, prior = use
                if not isinstance(prior, int) or prior > 0:
                    pe.wait_ge(free, prior)
                return bank

            def xnT_turn(n):
                for i in range(4):
                    use = t_use(("xnT", n, i))
                    bank = begin(use)
                    pe.wait_ge(xn_ready, NT * n + 2 * i + 2)
                    for t in range(2):
                        for k in range(KD):
                            mm = pe.transpose(bank[:, k * 256 + t * P:k * 256 + (t + 1) * P],
                                              xn[:, 2 * i + t, k * P:(k + 1) * P], ident[:, :])
                    mm.then_inc(use[1], 1)

            def xnT_wait(n, i):
                use = t_use(("xnT", n, i))
                pe.wait_ge(use[2], use[3] + 1)

            def bias(f, i):
                use = c_use(("bias", f, i))
                bank = begin(use)
                w = t_use(("wT", f, i // 2))
                pe.wait_ge(w[2], w[3] + 1)
                for t in range(2):
                    mm = pe.matmul(bank[:, t * O:(t + 1) * O], wT[:, (2 * i + t) * P:(2 * i + t + 1) * P],
                                   bexp[:, :], start=True, stop=True)
                mm.then_inc(use[1], 1)

            def ffn(f, n):
                use = m_use(("gate", f))
                bank = begin(use)
                pe.wait_ge(gate_in, 32)
                for t in range(NT):
                    if t % 2 == 0:
                        xnT_wait(n, t // 2)
                    for k in range(KD):
                        mm = pe.matmul(bank[:, t * E:(t + 1) * E], xnT[:, k, t * P:(t + 1) * P], wgate[:, k, :],
                                       start=(k == 0), stop=(k == KD - 1))
                mm.then_inc(use[1], 1)
                for t in range(NT):
                    for c in range(CHUNKS):
                        use = y_use(("y", f, t, c))
                        bank = begin(use)
                        if t == 0:
                            pe.wait_ge(wexp_in[c], 16)
                        for k in range(KD):
                            mm = pe.matmul(bank, xnT[:, k, t * P:(t + 1) * P], wexp[:, c, k, :],
                                           start=(k == 0), stop=(k == KD - 1))
                        mm.then_inc(use[1], 1)
                    if t == 1:
                        pe.wait_ge(wts_ready, f + 1)
                        for i in range(2):
                            use = t_use(("wT", f, i))
                            bank = begin(use)
                            for tt in range(4):
                                mm = pe.transpose(bank[0:E, tt * P:(tt + 1) * P], wts[:, 4 * i + tt, :], ident[:, :])
                            mm.then_inc(use[1], 1)
                    if t in (2, 4, 6):
                        bias(f, t // 2 - 1)
                bias(f, 3)

            pe.wait_ge(ident_made, 1)
            xnT_turn(0)
            ffn(0, 0)

            pe.wait_ge(absorb_in, 32)
            for i in range(4):
                use = yr.use(("absorb_k", i))
                bank = begin(use)
                k, half = i // 2, i % 2
                for n in range(8):
                    h = 8 * half + n
                    mm = pe.matmul(bank[0:QK, n * KV:(n + 1) * KV], wqcT[:, h, k * QK:(k + 1) * QK], wkcT[:, h, :],
                                   start=True, stop=True)
                mm.then_inc(use[1], 1)
            pe.wait_ge(wo_in, 32)
            for i in range(4):
                use = yr.use(("absorb_v", i))
                bank = begin(use)
                for n in range(2):
                    for h in range(2):
                        head = 4 * i + 2 * n + h
                        mm = pe.matmul(bank[64 * h:64 * h + 64, n * O:(n + 1) * O], wvT[:, head, :], wo[:, head, :],
                                       start=True, stop=True)
                mm.then_inc(use[1], 1)

            xnT_turn(1)
            pe.wait_ge(index_in, 16 * 6)
            for i in range(2):
                use = yr.use(("index_gate", i))
                bank = begin(use)
                xnT_wait(1, 2 * i)
                xnT_wait(1, 2 * i + 1)
                for k in range(KD):
                    mm = pe.matmul(bank[0:IH, :], widx_gate[:, k, :], xnT[:, k, BANK * i:BANK * (i + 1)],
                                   start=(k == 0), stop=(k == KD - 1))
                mm.then_inc(use[1], 1)
            pe.wait_ge(latent_in, 16 * 4)
            for i in range(2):
                use = yr.use(("latent_kv", i))
                bank = begin(use)
                for t in range(4):
                    for k in range(KD):
                        mm = pe.matmul(bank[:, t * P:(t + 1) * P], xnT[:, k, (4 * i + t) * P:(4 * i + t + 1) * P],
                                       wkv[:, k, :], start=(k == 0), stop=(k == KD - 1))
                mm.then_inc(use[1], 1)
            for i in range(4):
                use = yr.use(("latent_q", i))
                bank = begin(use)
                m, n = i // 2, i % 2
                for k in range(KD):
                    mm = pe.matmul(bank[0:QK, :], wcp[:, k, m * QK:(m + 1) * QK], xnT[:, k, BANK * n:BANK * (n + 1)],
                                   start=(k == 0), stop=(k == KD - 1))
                mm.then_inc(use[1], 1)
            for i in range(2):
                use = tr.use(("keysT", i))
                bank = begin(use)
                pe.wait_ge(key_roped, i + 1)
                for t in range(4):
                    mm = pe.transpose(bank[:, t * P:(t + 1) * P], kf[:, 4 * i + t, :], ident[:, :])
                mm.then_inc(use[1], 1)

            def index_step(name):
                use = cr.use((name,)) if (name,) in cr.at else mr.use((name,))
                return use, begin(use)

            def sel_onehot():
                use, bank = index_step("onehot")
                pe.wait_ge(hot_ready, 1)
                for t in range(NT):
                    mm = pe.transpose(bank[:, t * SEL:(t + 1) * SEL], hotT[:, t * P:(t + 1) * P], ident[0:SEL, 0:SEL])
                mm.then_inc(use[1], 1)

            def sel_rows():
                use, bank = index_step("rows")
                for k in range(KD):
                    for t in range(NT):
                        mm = pe.matmul(bank[:, k * SEL:(k + 1) * SEL], xn[:, t, k * P:(k + 1) * P], onehot[:, t, :],
                                       start=(t == 0), stop=(t == NT - 1))
                mm.then_inc(use[1], 1)

            def sel_states():
                use, bank = index_step("selected")
                for h in range(IH):
                    for k in range(KD):
                        mm = pe.matmul(bank[:, h * TOPK:(h + 1) * TOPK], widx[:, k, h * ID:(h + 1) * ID],
                                       rowsT[:, k, h * TOPK:(h + 1) * TOPK], start=(k == 0), stop=(k == KD - 1))
                mm.then_inc(use[1], 1)

            def sel_qkv():
                use, bank = index_step("sqkv")
                for w in range(2):
                    pe.matmul(bank[:, w * SEL:(w + 1) * SEL], ws3[:, w, :], selT, start=True, stop=True)
                pe.matmul(bank[0:SEL, P:2 * P], selT, ws3[:, 2, :], start=True, stop=True).then_inc(use[1], 1)

            def sel_scores():
                use, bank = index_step("sscores")
                pe.matmul(bank[0:SEL, 0:SEL], sqkT[:, 0, :], sqkT[:, 1, :], start=True, stop=True).then_inc(use[1], 1)

            def sel_mean():
                use, bank = index_step("smean")
                pe.wait_ge(sprob_ready, 1)
                pe.wait_ge(masks_made, 5)
                pe.matmul(bank[0:SEL, 0:IH], sprob, groups, start=True, stop=True).then_inc(use[1], 1)

            def sel_out():
                use, bank = index_step("sout")
                pe.matmul(bank[:, 0:IH], sv, smean, start=True, stop=True).then_inc(use[1], 1)

            def sel_io():
                use, bank = index_step("io")
                pe.matmul(bank[:, 0:IH], ws3[:, 3, :], soutT, start=True, stop=True).then_inc(use[1], 1)

            def sel_row():
                use, bank = index_step("io_row")
                last_c = cr.use(("io",))
                pe.wait_ge(last_c[2], last_c[3] + 1)
                pe.wait_ge(wosum_ready, 1)
                for h in range(IH):
                    mm = pe.matmul(bank[0:1, 0:O], ioT[:, h:h + 1], wosum[:, h, :], start=(h == 0), stop=(h == IH - 1))
                mm.then_inc(use[1], 1)

            def sel_all():
                use, bank = index_step("io_all")
                pe.matmul(bank[:, 0:O], ones[0:1, :], iorow[:, :], start=True, stop=True).then_inc(use[1], 1)

            for step in (sel_onehot, sel_rows, sel_states, sel_qkv, sel_scores, sel_mean, sel_out, sel_io,
                         sel_row, sel_all):
                step()

            def query(prior, pair, j):
                pe.wait_ge(m_free, prior)
                cols = wq[:, :, :, :].rearrange("p k h n -> p k (h n)")
                for k in range(2):
                    mm = pe.matmul(M[:, 0:2 * P], cpT[:, k, j * P:(j + 1) * P],
                                   cols[:, k, bass.ds(pair * 2 * P, 2 * P)], start=(k == 0), stop=(k == 1))
                mm.then_inc(m_full, 1)

            def query_turn(use, n, j):
                bank = begin(use)
                pe.wait_ge(query_roped, n + 1)
                for h in range(2):
                    mm = pe.transpose(bank[:, h * P:(h + 1) * P], qtok[:, j % 2, h, :], ident[:, :])
                mm.then_inc(use[1], 1)

            for key in [("latent_q", i) for i in range(4)]:
                use = yr.use(key)
                pe.wait_ge(use[2], use[3] + 1)
            for j in range(NT):
                query(mr.use(("query", j))[3], 0, j)
                if j:
                    query_turn(tr.use(("queryT", j - 1)), j - 1, j - 1)

            def scores(g, u):
                qt, h = u // 2, u % 2
                w = P * (qt + 1)
                s = S[u % 2]
                for c in range(0, w, BANK):
                    n = min(BANK, w - c)
                    mm = pe.matmul(s[:, c:c + n], qT[:, h, P * qt:P * (qt + 1)], keysT[:, c:c + n],
                                   start=True, stop=(c + n < w))
                pe.matmul(s[:, P * qt:w], identb[:, :], causal[:, :], start=False, stop=True) \
                    .then_inc(scores_ready, 1)

            def probs_turn(use, v, c):
                bank = begin(use)
                n = min(GT, tiles_of(v) - GT * c)
                for k in range(n):
                    kt = GT * c + k
                    mm = pe.transpose(bank[:, k * P:(k + 1) * P], probs[:, v % 4, kt * P:(kt + 1) * P], ident[:, :])
                mm.then_inc(use[1], 1)

            def sums_turn(use, n):
                bank = begin(use)
                pe.wait_ge(rwide_ready, n + 1)
                for t in range(GT):
                    mm = pe.transpose(bank[:, t * P:(t + 1) * P], rwide[:, t, :, :].rearrange("p h n -> p (h n)"), ident[:, :])
                mm.then_inc(use[1], 1)

            def pv(group, kt, prior):
                if kt == 0:
                    pe.wait_ge(c_free, prior)
                pT, kts = (pT0, GT) if group == 0 else (pT1, NT)
                q0 = max(0, kt - GT * group) * P
                for h in range(2):
                    mm = pe.matmul(C[64 * h:64 * h + 64, q0:BANK], kf[:, kt, 0:KV], pT[:, h, kt, q0:BANK],
                                   start=(kt == 0), stop=(kt == kts - 1))
                if kt == kts - 1:
                    mm.then_inc(c_full, 1)

            for i in range(4):
                pe.wait_ge(y_free[i], y_base)
            pe.wait_ge(tr.use(("keysT", 0))[2], tr.use(("keysT", 0))[3] + 1)
            pe.wait_ge(tr.use(("keysT", 1))[2], tr.use(("keysT", 1))[3] + 1)
            pe.wait_ge(masks_made, 5)

            def body(g):
                first, last = isinstance(g, int) and g == 0, isinstance(g, int) and g == PAIRS - 1
                items = turn_items(g)
                for u in range(UNITS):
                    if not first or u >= 2:
                        pe.wait_ge(probs_ready, UNITS * g + u - 1)
                    scores(g, u)
                    if u % 2 == 0 and not last:
                        query(m_query(g, u // 2), g + 1, u // 2)
                    for kind, args, b, prior in items[u]:
                        use = (TB[b], t_full[b], t_free[b], prior)
                        if kind == "probsT":
                            probs_turn(use, *args)
                        elif kind == "queryT":
                            j = args[0]
                            query_turn(use, NT * g + j if j == NT - 1 else NT * (g + 1) + j, j)
                        else:
                            sums_turn(use, 2 * g - 1 if args[0] == 1 else 2 * g)
                    if not first and PV_AT[1] <= u < PV_AT[1] + NT:
                        pv(1, u - PV_AT[1], c_group(g - 1, 1))
                    if PV_AT[0] <= u < PV_AT[0] + GT:
                        pv(0, u - PV_AT[0], c_group(g, 0))

            body(0)
            with pe.Fori(1, PAIRS - 1) as g:
                body(g)
            body(PAIRS - 1)

            def project(t):
                use = y_use(("project", t))
                bank = begin(use)
                for g in range(PAIRS):
                    mm = pe.matmul(bank[:, 0:O], ctxT[:, g, t * P:(t + 1) * P], absV[:, g, :],
                                   start=(g == 0), stop=(g == PAIRS - 1))
                mm.then_inc(use[1], 1)

            pe.wait_ge(probs_ready, UNITS * PAIRS)
            for v in (UNITS - 2, UNITS - 1):
                for c in range(chunks_of(v)):
                    probs_turn(t_use(("probsT", v, c)), v, c)
            pe.wait_ge(c_free, c_group(PAIRS - 1, 0) + 1)
            for t in range(GT):
                project(t)
            sums_turn(t_use(("sumsT", 1)), 2 * PAIRS - 1)
            for c in range(2):
                use = t_use(("probsT", UNITS - 1, c))
                pe.wait_ge(use[2], use[3] + 1)
            for kt in range(NT):
                pv(1, kt, c_group(PAIRS - 1, 1))
            pe.wait_ge(c_free, c_group(PAIRS - 1, 1) + 1)
            for t in range(GT, NT):
                project(t)
            xnT_turn(2)
            ffn(1, 2)

        @block.vector
        def _(dve):
            steps = [0]

            def settle(ins):
                ins.then_inc(dve_step, 1)
                steps[0] += 1
                dve.wait_ge(dve_step, steps[0])

            def tick(ins):
                ins.then_inc(dve_step, 1)
                steps[0] += 1

            def norm(n, half):
                ts = range(4 * half, 4 * half + 4)
                hs = slice(4 * half, 4 * half + 4)
                for t in ts:
                    if n == 0 and t % 2 == 0:
                        dve.wait_ge(x_in[t // 2], 16)
                    tick(dve.bn_stats(stats[:, t, :], x[:, t, :]))
                dve.wait_ge(dve_step, steps[0])
                for t in ts:
                    tick(dve.bn_aggr(mv[:, t, :], stats[:, t, :]))
                dve.wait_ge(dve_step, steps[0])
                dve.tensor_scalar(varE[:, hs], mv[:, hs, 1], EPS, None, ALU.add).then_inc(var_ready, 1)
                dve.wait_ge(sd_ready, 2 * n + half + 1)
                settle(dve.reciprocal(rs0[:, hs], sd[:, hs]))
                settle(dve.scalar_tensor_tensor(out=rs0[:, hs], in0=varE[:, hs], scalar=0.5, in1=rs0[:, hs],
                                                op0=ALU.mult, op1=ALU.mult))
                settle(dve.scalar_tensor_tensor(out=rs0[:, hs], in0=sd[:, hs], scalar=0.5, in1=rs0[:, hs],
                                                op0=ALU.mult, op1=ALU.add))
                settle(dve.reciprocal(rstd[:, hs], rs0[:, hs]))
                for t in ts:
                    dve.tensor_scalar(xn[:, t, :], x[:, t, :], mv[:, t, 0:1], rstd[:, t:t + 1],
                                      ALU.subtract, ALU.mult).then_inc(xn_ready, 1)

            def route(f):
                bank, full, free, prior = m_use(("gate", f))
                dve.wait_ge(full, prior + 1)
                dve.tensor_copy(logits[:, :, :], bank[:, 0:NT * E].rearrange("p (t e) -> p t e", t=NT)).then_inc(free, 1)
                dve.wait_ge(free, prior + 1)
                for t in range(NT):
                    tick(dve.max(top[:, t, :], logits[:, t, :]))
                dve.wait_ge(dve_step, steps[0])
                dve.tensor_tensor(gap[:, :], top[:, :, 1], top[:, :, 0], ALU.subtract).then_inc(gap_ready, 1)
                for t in range(NT):
                    tick(dve.max_index(topi[:, t, :], top[:, t, :], logits[:, t, :]))
                dve.wait_ge(dve_step, steps[0])
                settle(dve.tensor_copy(topf[:, :, :], topi[:, :, 0:2]))
                if f == 0:
                    dve.wait_ge(iotas_made, 1)
                for k in range(2):
                    tick(dve.tensor_tensor(hot[:, k, :, :], iota8[:, :, :],
                                           topf[:, :, k:k + 1].to_broadcast([P, NT, E]), ALU.is_equal))
                dve.wait_ge(egap_ready, f + 1)
                settle(dve.tensor_scalar(w2[:, :], egap[:, :], 2.0, 2.0, ALU.mult, ALU.add))
                settle(dve.reciprocal(w1[:, :], w2[:, :]))
                settle(dve.tensor_tensor(w2[:, :], w1[:, :], egap[:, :], ALU.mult))
                for k, w in enumerate((w1, w2)):
                    tick(dve.tensor_tensor(hot[:, k, :, :], hot[:, k, :, :],
                                           w[:, :].unsqueeze(2).to_broadcast([P, NT, E]), ALU.mult))
                dve.wait_ge(dve_step, steps[0])
                dve.tensor_tensor(wts[:, :, :], hot[:, 0, :, :], hot[:, 1, :, :], ALU.add).then_inc(wts_ready, 1)
                dve.wait_ge(wts_ready, f + 1)

            def combine(f, t):
                for c in range(CHUNKS):
                    bank, full, free, prior = y_use(("y", f, t, c))
                    dve.wait_ge(full, prior + 1)
                    for e in range(2):
                        ins = dve.scalar_tensor_tensor(out=x[:, t, :], in0=bank[:, e * O:(e + 1) * O],
                                                       scalar=wts[:, t, 2 * c + e:2 * c + e + 1], in1=x[:, t, :],
                                                       op0=ALU.mult, op1=ALU.add)
                        if e == 0:
                            settle(ins)
                        else:
                            ins.then_inc(free, 1)
                            dve.wait_ge(free, prior + 1)

            def add_bias(f, i):
                bank, full, free, prior = c_use(("bias", f, i))
                dve.wait_ge(full, prior + 1)
                ins = dve.tensor_tensor(x[:, 2 * i:2 * i + 2, :], bank[:, :].rearrange("p (t n) -> p t n", t=2),
                                        x[:, 2 * i:2 * i + 2, :], ALU.add)
                ins.then_inc(free, 1)
                dve.wait_ge(free, prior + 1)

            norm(0, 0)
            norm(0, 1)
            route(0)
            for t in range(NT):
                combine(0, t)
                if t in (2, 4, 6):
                    add_bias(0, t // 2 - 1)
                if t == 4:
                    norm(1, 0)
            add_bias(0, 3)
            norm(1, 1)

            def take(name, dst, src):
                bank, full, free, prior = cr.use((name,)) if (name,) in cr.at else mr.use((name,))
                dve.wait_ge(full, prior + 1)
                dve.tensor_copy(dst, src(bank)).then_inc(free, 1)

            for i in range(2):
                use = yr.use(("index_gate", i))
                dve.wait_ge(use[2], use[3] + 1)
            settle(dve.max(gtop, gT))
            settle(dve.max_index(gidx, gtop, gT))
            dve.tensor_copy(gidf, gidx).then_inc(index_listed, 1)
            dve.wait_ge(index_spread, 16)
            dve.wait_ge(iotas_made, 2)
            dve.tensor_scalar(hotT, iotaT, idxp, None, ALU.is_equal).then_inc(hot_ready, 1)
            take("onehot", onehot, lambda b: b[:, :].rearrange("p (t s) -> p t s", t=NT))
            take("rows", rowsT, lambda b: b[:, 0:KD * SEL].rearrange("p (k s) -> p k s", k=KD))
            take("selected", selT, lambda b: b[:, 0:SEL])
            bank, full, free, prior = cr.use(("sqkv",))
            dve.wait_ge(full, prior + 1)
            tick(dve.tensor_copy(sv, bank[0:SEL, P:2 * P]))
            dve.tensor_copy(sqkT, bank[:, 0:2 * SEL].rearrange("p (w s) -> p w s", w=2)).then_inc(free, 1)
            bank, full, free, prior = cr.use(("sscores",))
            dve.wait_ge(full, prior + 1)
            dve.wait_ge(masks_made, 5)
            dve.scalar_tensor_tensor(out=ssc, in0=bank[0:SEL, 0:SEL], scalar=1.0 / float(np.sqrt(ID)), in1=blockmask,
                                     op0=ALU.mult, op1=ALU.add).then_inc(free, 1)
            dve.wait_ge(free, prior + 1)
            dve.tensor_reduce(snm, ssc, AX.X, ALU.max, negate=True).then_inc(sscore_ready, 1)
            dve.wait_ge(sexp_ready, 1)
            settle(dve.reciprocal(srs, ssum))
            dve.tensor_scalar(sprob, sp_, srs, None, ALU.mult).then_inc(sprob_ready, 1)
            take("smean", smean, lambda b: b[0:SEL, 0:IH])
            take("sout", soutT, lambda b: b[:, 0:IH])
            take("io", ioT, lambda b: b[:, 0:IH])
            take("io_row", iorow[:, :], lambda b: b[0:1, 0:O])
            bank, full, free, prior = mr.use(("io_all",))
            dve.wait_ge(full, prior + 1)
            dve.tensor_tensor(x[:, :, :], x[:, :, :], bank[:, 0:O].unsqueeze(1).to_broadcast([P, NT, O]), ALU.add) \
                .then_inc(free, 1)

            def drain(use, dst, src_of):
                bank, full, free, prior = use
                dve.wait_ge(full, prior + 1)
                dve.tensor_copy(dst, src_of(bank)).then_inc(free, 1)

            def group_sums(group, n):
                dve.wait_ge(probs_ready, n)
                dve.reciprocal(rsum[:, group, :, :], sums[:, group, :, :]).then_inc(rsum_ready, 1)

            def context(g, group, prior, r_use):
                dve.wait_ge(c_full, prior + 1)
                dve.wait_ge(r_use[2], r_use[3] + 1)
                flat = ctxT[:, :, :].rearrange("p g n -> p (g n)")
                dve.tensor_tensor(flat[:, bass.ds(g * T + group * BANK, BANK)], C[:, :], rT[:, group, :], ALU.mult) \
                    .then_inc(c_free, 1)

            def sums_use(items, group):
                (kind, args, b, prior), = [i for i in items[R_AT[group]] if i[0] == "sumsT"]
                return TB[b], t_full[b], t_free[b], prior

            def body(g):
                first = isinstance(g, int) and g == 0
                items = turn_items(g)
                for u in range(UNITS):
                    qt = u // 2
                    dve.wait_ge(scores_ready, UNITS * g + u + 1)
                    dve.tensor_reduce(negmax[:, u % 4:u % 4 + 1], S[u % 2][:, 0:P * (qt + 1)], AX.X, ALU.max,
                                      negate=True).then_inc(negmax_ready, 1)
                    if u == 0 and not first:
                        b0 = sums_before(g)
                        context(g - 1, 0, c_group(g - 1, 0), b0)
                    for kind, args, b, prior in items[u]:
                        if kind == "probsT" and args[1] == 0:
                            probsT_drain(drain, (TB[b], t_full[b], t_free[b], prior), *args)
                    if u == 1 and not first:
                        group_sums(1, UNITS * g)
                    if u == 9:
                        group_sums(0, UNITS * g + 8)
                    if u == PV_AT[1] + NT and not first:
                        context(g - 1, 1, c_group(g - 1, 1), sums_use(items, 1))

            def sums_before(g):
                if isinstance(g, int):
                    return sums_use(turn_items(g - 1), 0)
                return sums_use(turn_items(g - 1), 0)

            body(0)
            with dve.Fori(1, PAIRS - 1) as g:
                body(g)
            body(PAIRS - 1)
            group_sums(1, UNITS * PAIRS)
            context(PAIRS - 1, 0, c_group(PAIRS - 1, 0), sums_before(PAIRS))
            for v in (UNITS - 2, UNITS - 1):
                probsT_drain(drain, t_use(("probsT", v, 0)), v, 0)

            def residual(t):
                bank, full, free, prior = y_use(("project", t))
                dve.wait_ge(full, prior + 1)
                ins = dve.tensor_tensor(x[:, t, :], bank[:, 0:O], x[:, t, :], ALU.add)
                ins.then_inc(free, 1)
                dve.wait_ge(free, prior + 1)

            for t in range(GT):
                residual(t)
            norm(2, 0)
            last_r = t_use(("sumsT", 1))
            context(PAIRS - 1, 1, c_group(PAIRS - 1, 1), last_r)
            for t in range(GT, NT):
                residual(t)
            norm(2, 1)
            route(1)
            for t in range(NT):
                combine(1, t)
                if t in (2, 4, 6):
                    add_bias(1, t // 2 - 1)
            add_bias(1, 3)


def kernel(L0_attn_x, L0_attn_W_c, L0_attn_W_cp, L0_attn_W_qc, L0_attn_W_qr, L0_attn_W_kc, L0_attn_W_kr, L0_attn_W_v,
           L0_attn_W_o, L0_attn_W_idx, L0_attn_W_gate, L0_attn_W_sq, L0_attn_W_sk, L0_attn_W_sv, L0_attn_W_iout,
           L0_ffn_gate_w, L0_ffn_expert_w, L0_ffn_expert_b):
    import concourse.bacc as bacc
    from concourse.bass_utils import run_bass_kernel_spmd

    halves = np.concatenate([np.arange(0, DR, 2), np.arange(1, DR, 2)])
    inv = 1.0 / 10000.0 ** (np.arange(0, DR, 2)[:DR // 2].astype(np.float32) / DR)
    freqs = np.outer(np.arange(T, dtype=np.float32), inv)
    cos, sin = np.cos(freqs).astype(np.float32), np.sin(freqs).astype(np.float32)

    def np_(v):
        return np.asarray(v)

    def tiles(v, p):
        v = np_(v)
        return v.reshape(v.shape[0] // p, p, -1).transpose(1, 0, 2)

    data = {
        "x": np_(L0_attn_x).reshape(T, D),
        "gate_w": tiles(np_(L0_ffn_gate_w).T, P),
        "expert_b": np_(L0_ffn_expert_b),
        "expert_w": np_(L0_ffn_expert_w).reshape(CHUNKS, 2, O, KD, P).transpose(4, 0, 3, 1, 2).reshape(P, CHUNKS, KD, 2 * O),
        "W_qc": np_(L0_attn_W_qc).reshape(QL, NH, DK).transpose(2, 1, 0),
        "W_kc": np_(L0_attn_W_kc).reshape(KV, NH, DK).transpose(2, 1, 0),
        "W_v": np_(L0_attn_W_v).reshape(KV, NH, DV).transpose(2, 1, 0),
        "W_o": np_(L0_attn_W_o).reshape(NH, DV, D).transpose(1, 0, 2),
        "W_qr": np_(L0_attn_W_qr).reshape(2, QK, NH, DR)[..., halves].transpose(1, 0, 2, 3),
        "W_cp": tiles(L0_attn_W_cp, P),
        "W_c": tiles(L0_attn_W_c, P),
        "W_kr": tiles(np_(L0_attn_W_kr)[:, halves], P),
        "cos": tiles(np.concatenate([cos, cos], axis=1), P),
        "sin": tiles(np.concatenate([-sin, sin], axis=1), P),
        "W_idx": tiles(L0_attn_W_idx, P),
        "W_gate": tiles(L0_attn_W_gate, P),
        "W_sq": np_(L0_attn_W_sq),
        "W_sk": np_(L0_attn_W_sk),
        "W_sv": np_(L0_attn_W_sv),
        "W_iout": np_(L0_attn_W_iout)[:, 0:DV],
    }
    nc = bacc.Bacc("TRN2", target_bir_lowering=False, num_devices=1)
    arrays, a = {}, {}
    for name, v in data.items():
        v = np.ascontiguousarray(v)
        arrays[f"in_{name}"] = v
        a[name] = nc.dram_tensor(f"in_{name}", v.shape, mybir.dt.from_np(v.dtype), kind="ExternalInput").ap()
    out = nc.dram_tensor("out", (T, D), F32, kind="ExternalOutput").ap()
    build(nc, a, out)
    r = run_bass_kernel_spmd(nc, [arrays], core_ids=[0])
    return r.results[0]["out"].reshape(1, T, D)
```

```python
import numpy as np
import concourse.bass as bass
from concourse import mybir
from contextlib import ExitStack

F32 = mybir.dt.float32
F32R = mybir.dt.float32r
BF16 = mybir.dt.bfloat16
U32 = mybir.dt.uint32
ALU = mybir.AluOpType
ACT = mybir.ActivationFunctionType
AX = mybir.AxisListType

P = 128
T, D = 1024, 256
NT, KD = T // P, D // P
E, O = 8, 256
CHUNKS = E // 2
NH, DK, DR, DV = 16, 128, 64, 128
KV, QL = 64, 192
QK = QL // 2
PAIRS = NH // 2
IH, ID, TOPK = 8, 128, 8
SEL = IH * TOPK
GT = 4
SCALE = 1.0 / float(np.sqrt(DK + DR))
EPS = 1e-5
MASK_ON_DVE = 4
MASKED = -1e30
BANK = 512


class Ring:

    def __init__(self, banks, full, free, order):
        self.banks, self.full, self.free = banks, full, free
        self.at = {key: i for i, key in enumerate(order)}
        self.n = len(order)

    def use(self, key):
        i = self.at[key]
        b = i % len(self.banks)
        return self.banks[b], self.full[b], self.free[b], i // len(self.banks)


UNITS = 2 * NT
LAG = 2
Q_LAG = 5
Q_LATE = (UNITS - Q_LAG) // 2 + 1
Q_SLOTS = 4
SEXP_AT = 5
R_AT = {1: 6, 0: 14}
PV_AT = {1: 4, 0: UNITS - 2}
PV0_LATE = GT - (UNITS - PV_AT[0])

Y_ORDER = [("y", 0, t, c) for t in range(NT) for c in range(CHUNKS)] \
    + [("absorb_k", i) for i in range(4)] + [("absorb_v", i) for i in range(4)] \
    + [(name, *i) for half in range(2)
       for name, i in (("index_gate", (half,)), ("latent_kv", (half,)), ("latent_q", (0, half)), ("latent_q", (1, half)))]
Y_TAIL = [("project", t) for t in range(NT)] \
    + [("y", 1, t, c) for t in range(NT) for c in range(CHUNKS)]
def ffn_turns(f, n):
    return [("xnT", n, 0), ("xnT", n, 1), ("wT", f, 0), ("xnT", n, 2), ("xnT", n, 3), ("wT", f, 1)]


T_ORDER = ffn_turns(0, 0) + [("xnT", 1, i) for i in range(4)] + [("keysT", i) for i in range(2)] \
    + [("queryT", j) for j in range(Q_LATE)]
M_ORDER = [("gate", 0, 0), ("gate", 0, 1)] + [("query", j) for j in range(NT)]
C_ORDER = [("bias", 0, i) for i in range(4)] \
    + [(s,) for s in ("onehot", "rows", "selected", "sqkv", "sscores", "smean", "sout", "io", "io_row", "io_all")]

def tiles_of(v):
    return v // 2 + 1


def chunks_of(v):
    return (tiles_of(v) + GT - 1) // GT


def loop_items():
    items = []
    for u in range(UNITS):
        v = (u - LAG) % UNITS
        items += [(u, "probsT", (v, c), u < LAG) for c in range(chunks_of(v))]
        if u % 2 == 1:
            j = (u - Q_LAG) // 2 % NT
            items.append((u, "queryT", (j,), False))
        for group, at in R_AT.items():
            if at == u:
                items.append((u, "sumsT", (group,), group == 1))
    return items


LOOP_ITEMS = loop_items()
assert len(LOOP_ITEMS) % 2 == 0


def turn_items(g, pair_count=PAIRS):
    first, last = isinstance(g, int) and g == 0, isinstance(g, int) and g == pair_count - 1
    base = len(T_ORDER)
    before = [len([i for i in range(base) if i % 2 == b]) for b in range(2)]
    missing = [len([1 for n, it in enumerate(LOOP_ITEMS) if it[3] and (base + n) % 2 == b]) for b in range(2)]
    count, out = [0, 0], {u: [] for u in range(UNITS)}
    for n, (u, kind, args, needs_earlier) in enumerate(LOOP_ITEMS):
        if first and needs_earlier:
            continue
        if last and kind == "queryT" and args[0] < Q_LATE:
            continue
        b = (base + n) % 2
        start = before[b] if first else before[b] - missing[b] + g * (len(LOOP_ITEMS) // 2)
        out[u].append((kind, args, b, start + count[b]))
        count[b] += 1
    return out


def turn_tail():
    last = turn_items(PAIRS - 1)
    seen = [0, 0]
    for items in last.values():
        for _, _, b, prior in items:
            seen[b] = prior + 1
    order = [("probsT", v, c) for v in (UNITS - 2, UNITS - 1) for c in range(chunks_of(v))] \
        + [("sumsT", 1)] + ffn_turns(1, 2)
    out = {}
    for i, key in enumerate(order):
        out[key] = (i % 2, seen[i % 2])
        seen[i % 2] += 1
    return out


def build(nc, a, out):
    ctx = ExitStack()
    with ctx:
        def sb(name, shape, dt=F32):
            return ctx.enter_context(nc.sbuf_tensor(name, shape, dt))

        def sb_over(name, shape, base, dt=F32R):
            return nc.alloc_sbuf_tensor_at(name, shape, dt, offset=base)

        def base():
            return (nc.sbuf_base + 31) // 32 * 32

        def sem(name):
            return ctx.enter_context(nc.semaphore(name))

        x = sb("x", [P, NT, D])
        whi = sb("whi", [P, CHUNKS, KD, 2 * O], F32R)
        wgate = sb("wgate", [P, KD, E])
        bexp = sb("bexp", [E, O])
        wts = sb("wts", [P, NT, E])
        wT = sb("wT", [E, T])
        stats = sb("stats", [P, NT, 6])
        mv = sb("mv", [P, NT, 2])
        varE = sb("varE", [P, NT])
        sd = sb("sd", [P, NT])
        rs0 = sb("rs0", [P, NT])
        rstd = sb("rstd", [P, NT])
        logits = sb("logits", [P, NT, E])
        top = sb("top", [P, NT, 8])
        topi = sb("topi", [P, NT, 8], U32)
        topf = sb("topf", [P, NT, 2])
        gap = sb("gap", [P, NT])
        egap = sb("egap", [P, NT])
        w1 = sb("w1", [P, NT])
        w2 = sb("w2", [P, NT])
        hot = sb("hot", [P, 2, NT, E])
        iota8 = sb("iota8", [P, NT, E])

        wq_room = sb("wq_room", [P, 2 * NH * P])
        wq = wq_room[0:QK, :].rearrange("p (k h n) -> p k h n", k=2, h=NH)
        wraw = wq_room[:, :].rearrange("p (c k n) -> p c k n", c=CHUNKS, k=KD)
        wcp = sb("wcp", [P, KD, QL])
        wkv = sb("wkv", [P, KD, P])
        widx_gate = sb("widx_gate", [P, KD, IH])
        cpT_room = sb("cpT_room", [P, 2, T])
        cpT = cpT_room[0:QK, :, :]
        xraw = cpT_room[:, :, :]
        kf = sb("kf", [P, NT, P])
        keysT = sb("keysT", [P, T])
        qtok = sb("qtok", [P, Q_SLOTS, 2, P])
        ropeA = sb("ropeA", [P, 4, DR])
        ropeB = sb("ropeB", [P, 4, DR])
        cosT = sb("cosT", [P, NT, DR])
        sinT = sb("sinT", [P, NT, DR])
        qT_base = base()
        qT = sb("qT", [P, 2, T])
        probs_base = base()
        probs = sb("probs", [P, 4, T])
        xn = probs[:, 0:2, :].rearrange("p a (t n) -> p (a t) n", n=D)
        xnT = probs[:, 2:4, :]
        xhi = sb_over("xhi", [P, KD, T], probs_base + 2 * T * 4)
        xlo = sb_over("xlo", [P, KD, T], qT_base)
        pT0_base = base()
        pT0 = sb("pT0", [P, 2, GT, BANK])
        pT1 = sb("pT1", [P, 2, NT, BANK])
        ctxT_base = base()
        ctxT = sb("ctxT", [P, PAIRS, T])
        absV = sb("absV", [P, PAIRS, O])
        negmax = sb("negmax", [P, 4])
        sums = sb("sums", [P, 2, GT, 2])
        rsum = sb("rsum", [P, 2, GT, 2])
        rwide = sb("rwide", [P, GT, 2, 64])
        rT = sb("rT", [P, 2, BANK])
        ident = sb("ident", [P, P])
        identb = sb("identb", [P, P], BF16)
        causal = sb("causal", [P, P], BF16)
        ones = sb("ones", [P, P])
        iorow = sb("iorow", [1, O])

        early1 = pT1[:, :, :, :].rearrange("p h k n -> p (h k n)")
        wlo = [sb_over(f"wlo{f}", [P, CHUNKS, KD, 2 * O], at) for f, at in enumerate((ctxT_base, pT0_base))]
        wo = early1[:, 0:4096].rearrange("p (h n) -> p h n", h=NH)
        wvT = early1[:, 4096:5120].rearrange("p (h n) -> p h n", h=NH)
        wkcT = early1[:, 5120:6144].rearrange("p (h n) -> p h n", h=NH)
        wosum = early1[:, 6144:8192].rearrange("p (h n) -> p h n", h=IH)
        early0 = pT0[:, :, :, :].rearrange("p h k n -> p (h k n)")
        wqcT = early0[:, 0:3072].rearrange("p (h n) -> p h n", h=NH)
        ws3 = early0[:, 3072:3584].rearrange("p (w n) -> p w n", w=4)
        early2 = ctxT[:, :, :].rearrange("p g n -> p (g n)")
        widx = early2[:, 0:2048].rearrange("p (k n) -> p k n", k=KD)
        iotaT = early2[0:SEL, 2048:3072]
        hotT = early2[0:SEL, 3072:4096]
        onehot = early2[:, 4096:4608].rearrange("p (t s) -> p t s", t=NT)
        gT = early2[0:IH, 4608:5632]
        rowsT = early2[:, 5632:5760].rearrange("p (k s) -> p k s", k=KD)
        selT = early2[:, 5760:5824]
        sqkT = early2[:, 5824:5952].rearrange("p (w s) -> p w s", w=2)
        sv = early2[0:SEL, 5952:6080]
        blockmask = early2[0:SEL, 6080:6144]
        groups = early2[0:SEL, 6144:6152]
        ssc = early2[0:SEL, 6152:6216]
        sp_ = early2[0:SEL, 6216:6280]
        smean = early2[0:SEL, 6280:6288]
        soutT = early2[:, 6288:6296]
        ioT = early2[:, 6296:6304]
        gtop = early2[0:IH, 6304:6312]
        gidx = early2[0:IH, 6312:6320].bitcast(U32)
        gidf = early2[0:IH, 6320:6328]
        idxp = early2[0:SEL, 6328:6329]
        snm = early2[0:SEL, 6329:6330]
        ssum = early2[0:SEL, 6330:6331]
        srs = early2[0:SEL, 6331:6332]
        sprob = early2[0:SEL, 6336:6400]

        S = [ctx.enter_context(nc.psum_tensor(f"S{i}", [P, 2 * BANK], F32)) for i in range(2)]
        TB = [ctx.enter_context(nc.psum_tensor(f"TB{i}", [P, BANK], F32)) for i in range(2)]
        M = ctx.enter_context(nc.psum_tensor("M", [P, BANK], F32))
        C = ctx.enter_context(nc.psum_tensor("C", [P, BANK], F32))
        YB = [S[i // 2][:, (i % 2) * BANK:(i % 2 + 1) * BANK] for i in range(4)]

        x_in = [sem(f"x_in{i}") for i in range(4)]
        wexp_in = [sem(f"wexp_in{i}") for i in range(CHUNKS)]
        wexp_again = [sem(f"wexp_again{i}") for i in range(CHUNKS)]
        whi_ready, wlo_ready, xhi_ready, xlo_ready = sem("whi_ready"), sem("wlo_ready"), sem("xhi_ready"), sem("xlo_ready")
        masked = sem("masked")
        gate_in, latent_in, absorb_in, rope_in = sem("gate_in"), sem("latent_in"), sem("absorb_in"), sem("rope_in")
        wo_in, index_in = sem("wo_in"), sem("index_in")
        ident_made, masks_made, iotas_made = sem("ident_made"), sem("masks_made"), sem("iotas_made")
        pool_step = sem("pool_step")
        dve_step = sem("dve_step")
        var_ready, sd_ready, xn_ready = sem("var_ready"), sem("sd_ready"), sem("xn_ready")
        gap_ready, egap_ready, wts_ready = sem("gap_ready"), sem("egap_ready"), sem("wts_ready")
        y_full, y_free = [sem(f"y_full{i}") for i in range(4)], [sem(f"y_free{i}") for i in range(4)]
        t_full, t_free = [sem(f"t_full{i}") for i in range(2)], [sem(f"t_free{i}") for i in range(2)]
        m_full, m_free, c_full, c_free = sem("m_full"), sem("m_free"), sem("c_full"), sem("c_free")
        index_listed, index_spread, hot_ready = sem("index_listed"), sem("index_spread"), sem("hot_ready")
        sscore_ready, sexp_ready, sprob_ready = sem("sscore_ready"), sem("sexp_ready"), sem("sprob_ready")
        wosum_ready = sem("wosum_ready")
        key_roped = sem("key_roped")
        query_roped = sem("query_roped")
        scores_ready, negmax_ready, probs_ready = sem("scores_ready"), sem("negmax_ready"), sem("probs_ready")
        rsum_ready, rwide_ready = sem("rsum_ready"), sem("rwide_ready")
        out_done = sem("out_done")

        yr = Ring(YB, y_full, y_free, Y_ORDER)
        tr = Ring([TB[0], TB[1]], t_full, t_free, T_ORDER)
        mr = Ring([M], [m_full], [m_free], M_ORDER)
        cr = Ring([C], [c_full], [c_free], C_ORDER)
        y_base = len(Y_ORDER) // 4
        tail = turn_tail()

        def y_use(key):
            if key in yr.at:
                return yr.use(key)
            i = Y_TAIL.index(key)
            return YB[i % 4], y_full[i % 4], y_free[i % 4], y_base + i // 4

        def t_use(key):
            if key in tr.at:
                return tr.use(key)
            b, prior = tail[key]
            return TB[b], t_full[b], t_free[b], prior

        def m_use(key):
            if key in mr.at:
                return mr.use(key)
            return M, m_full, m_free, mr.n + (PAIRS - 1) * NT + key[2]

        def c_use(key):
            if key in cr.at:
                return cr.use(key)
            return C, c_full, c_free, cr.n + 2 * PAIRS + key[2]

        def m_query(g, j):
            return mr.n + g * NT + j

        def c_group(g, group):
            return cr.n + 2 * g + group

        def probsT_drain(drain, use, v, c):
            qt, h = v // 2, v % 2
            n = min(GT, tiles_of(v) - GT * c)
            pT = pT0 if qt < GT else pT1
            drain(use, pT[:, h, GT * c:GT * c + n, P * (qt % GT):P * (qt % GT + 1)],
                  lambda b: b[:, 0:n * P].rearrange("p (k n) -> p k n", k=n))

        block = ctx.enter_context(nc.Block())

        @block.sync
        def _(sp):
            x_v = a["x"].rearrange("(t p) n -> p t n", p=P)
            for i in range(4):
                sp.dma_start(x[:, 2 * i:2 * i + 2, :], x_v[:, 2 * i:2 * i + 2, :]).then_inc(x_in[i], 16)
            sp.dma_start(wgate[:, :, :], a["gate_w"]).then_inc(gate_in, 16)
            sp.dma_start(bexp[:, :], a["expert_b"]).then_inc(gate_in, 16)
            for c in range(CHUNKS):
                sp.dma_start(wraw[:, c, :, :], a["expert_w"][:, c, :, :]).then_inc(wexp_in[c], 16)
            sp.dma_start(wqcT, a["W_qc"]).then_inc(absorb_in, 16)
            sp.dma_start(wkcT, a["W_kc"]).then_inc(absorb_in, 16)
            sp.dma_start(wvT, a["W_v"]).then_inc(wo_in, 16)
            sp.dma_start(wo, a["W_o"]).then_inc(wo_in, 16)
            sp.wait_ge(wlo_ready, CHUNKS)
            sp.dma_start(wq[:, :, :, KV:P], a["W_qr"]).then_inc(latent_in, 16)
            sp.dma_start(wcp[:, :, :], a["W_cp"]).then_inc(latent_in, 16)
            sp.dma_start(wkv[:, :, 0:KV], a["W_c"]).then_inc(latent_in, 16)
            sp.dma_start(wkv[:, :, KV:P], a["W_kr"]).then_inc(latent_in, 16)
            sp.dma_start(cosT[:, :, :], a["cos"]).then_inc(rope_in, 16)
            sp.dma_start(sinT[:, :, :], a["sin"]).then_inc(rope_in, 16)
            use = y_use(("y", 0, NT - 1, CHUNKS - 1))
            sp.wait_ge(use[1], use[3] + 1)
            sp.dma_start(widx, a["W_idx"]).then_inc(index_in, 16)
            sp.dma_start(widx_gate[:, :, :], a["W_gate"]).then_inc(index_in, 16)
            for n, name in enumerate(("W_sq", "W_sk", "W_sv", "W_iout")):
                sp.dma_start(ws3[:, n, :], a[name]).then_inc(index_in, 16)
            sp.wait_ge(index_listed, 1)
            sp.dma_start(idxp, gidf).then_inc(index_spread, 16)
            sp.wait_ge(m_full, mr.n + (PAIRS - 1) * NT)
            for c in range(CHUNKS):
                sp.dma_start(wraw[:, c, :, :], a["expert_w"][:, c, :, :]).then_inc(wexp_again[c], 16)
            out_v = out.rearrange("(t p) n -> p t n", p=P)
            for i in range(4):
                use = c_use(("bias", 1, i))
                sp.wait_ge(use[2], use[3] + 1)
                sp.dma_start(out_v[:, 2 * i:2 * i + 2, :], x[:, 2 * i:2 * i + 2, :]).then_inc(out_done, 16)
            sp.wait_ge(out_done, 16 * 4)

        @block.gpsimd
        def _(pool):
            steps = [0]

            def settle(ins):
                ins.then_inc(pool_step, 1)
                steps[0] += 1
                pool.wait_ge(pool_step, steps[0])

            settle(pool.memset(ident[:, :], 0.0))
            pool.affine_select(out=ident[:, :], in_=ident[:, :], compare_op=ALU.not_equal, fill=1.0, base=0,
                               pattern=[[-1, P]], channel_multiplier=1).then_inc(ident_made, 1)
            pool.iota(iota8[:, :, :], [[0, NT], [1, E]], base=0, channel_multiplier=0,
                      allow_small_or_imprecise_dtypes=True).then_inc(iotas_made, 1)
            def low_activations(f, i):
                pool.wait_ge(xhi_ready, 4 * f + i + 1)
                cols = slice(256 * i, 256 * i + 256)
                pool.tensor_tensor(xlo[:, :, cols], xraw[:, :, cols], xhi[:, :, cols].bitcast(F32), ALU.subtract) \
                    .then_inc(xlo_ready, 1)

            def low_weights(f, c, loaded):
                pool.wait_ge(loaded[c], 16)
                if f == 0:
                    pool.wait_ge(whi_ready, c + 1)
                pool.tensor_tensor(wlo[f][:, c, :, :], wraw[:, c, :, :], whi[:, c, :, :].bitcast(F32), ALU.subtract) \
                    .then_inc(wlo_ready, 1)

            low_activations(0, 0)
            low_weights(0, 0, wexp_in)
            low_weights(0, 1, wexp_in)
            low_activations(0, 1)
            low_weights(0, 2, wexp_in)
            low_weights(0, 3, wexp_in)
            low_activations(0, 2)
            low_activations(0, 3)
            pool.wait_ge(ident_made, 1)
            pool.tensor_copy(identb[:, :], ident[:, :]).then_inc(masks_made, 1)
            settle(pool.memset(causal[:, :], 0.0))
            pool.affine_select(out=causal[:, :], in_=causal[:, :], compare_op=ALU.is_ge, fill=MASKED, base=0,
                               pattern=[[-1, P]], channel_multiplier=1).then_inc(masks_made, 1)
            pool.memset(ones[:, :], 1.0).then_inc(masks_made, 1)
            use = y_use(("y", 0, NT - 1, CHUNKS - 1))
            pool.wait_ge(use[1], use[3] + 1)
            pool.iota(iotaT, [[1, T]], base=0, channel_multiplier=0,
                      allow_small_or_imprecise_dtypes=True).then_inc(iotas_made, 1)
            settle(pool.memset(blockmask, 0.0))
            bm = blockmask.rearrange("p (h j) -> p h j", h=IH)
            settle(pool.affine_select(out=bm, in_=bm, compare_op=ALU.is_ge, fill=MASKED, base=0,
                                      pattern=[[-TOPK, IH], [0, TOPK]], channel_multiplier=1))
            pool.affine_select(out=bm, in_=bm, compare_op=ALU.is_ge, fill=MASKED, base=TOPK - 1,
                               pattern=[[TOPK, IH], [0, TOPK]], channel_multiplier=-1).then_inc(masks_made, 1)
            settle(pool.memset(groups, 1.0 / TOPK))
            settle(pool.affine_select(out=groups, in_=groups, compare_op=ALU.is_ge, fill=0.0, base=0,
                                      pattern=[[-TOPK, IH]], channel_multiplier=1))
            pool.affine_select(out=groups, in_=groups, compare_op=ALU.is_ge, fill=0.0, base=TOPK - 1,
                               pattern=[[TOPK, IH]], channel_multiplier=-1).then_inc(masks_made, 1)
            pool.wait_ge(wo_in, 32)
            wo_p = wo.rearrange("p (i two) n -> p i two n", two=2)
            pool.tensor_tensor(wosum, wo_p[:, :, 0, :], wo_p[:, :, 1, :], ALU.add).then_inc(wosum_ready, 1)

            def rope(view, cos, sin, n, done):
                h = DR // 2
                pool.tensor_tensor(ropeA[:, 0:n, :], view, cos, ALU.mult).then_inc(pool_step, 1)
                pool.tensor_tensor(ropeB[:, 0:n, 0:h], view[:, :, h:DR], sin[:, :, 0:h], ALU.mult).then_inc(pool_step, 1)
                pool.tensor_tensor(ropeB[:, 0:n, h:DR], view[:, :, 0:h], sin[:, :, h:DR], ALU.mult).then_inc(pool_step, 1)

            def rope_add(view, n, done):
                pool.tensor_tensor(view, ropeA[:, 0:n, :], ropeB[:, 0:n, :], ALU.add).then_inc(done, 1)

            pool.wait_ge(rope_in, 32)
            for i in range(2):
                view = kf[:, 4 * i:4 * i + 4, KV:P]
                use = yr.use(("latent_kv", i))
                pool.wait_ge(use[2], use[3] + 1)
                if i:
                    pool.wait_ge(key_roped, i)
                rope(view, cosT[:, 4 * i:4 * i + 4, :], sinT[:, 4 * i:4 * i + 4, :], 4, key_roped)
                steps[0] += 3
                pool.wait_ge(pool_step, steps[0])
                rope_add(view, 4, key_roped)
            pool.wait_ge(key_roped, 2)
            step_base = steps[0]

            def query_rope(n, j):
                view = qtok[:, j % Q_SLOTS, :, KV:P]
                tab = [t[:, j, :].unsqueeze(1).to_broadcast([P, 2, DR]) for t in (cosT, sinT)]
                pool.wait_ge(m_free, mr.at[("query", 0)] + 1 + n)
                if not isinstance(n, int) or n > 0:
                    pool.wait_ge(query_roped, n)
                rope(view, tab[0], tab[1], 2, query_roped)
                pool.wait_ge(pool_step, step_base + 3 + 3 * n)
                rope_add(view, 2, query_roped)

            def spread(n, group):
                pool.wait_ge(rsum_ready, n + 1)
                wide = rsum[:, group, :, :].unsqueeze(3).to_broadcast([P, GT, 2, 64])
                one = ones[:, 0:1].unsqueeze(2).unsqueeze(3).to_broadcast([P, GT, 2, 64])
                pool.tensor_tensor(rwide[:, :, :, :], wide, one, ALU.mult).then_inc(rwide_ready, 1)

            for j in range(NT):
                query_rope(j, j)

            def body(g):
                last = isinstance(g, int) and g == PAIRS - 1
                first = isinstance(g, int) and g == 0
                for u in range(UNITS):
                    if u == 1 and not first:
                        spread(2 * g - 1, 1)
                    if u == 9:
                        spread(2 * g, 0)
                    if u % 2 == 0 and not last:
                        query_rope(NT + g * NT + u // 2, u // 2)

            body(0)
            with pool.Fori(1, PAIRS - 1) as g:
                body(g)
            body(PAIRS - 1)
            spread(2 * PAIRS - 1, 1)
            pool.wait_ge(c_full, c_group(PAIRS - 1, 0) + 1)
            for c in range(CHUNKS):
                low_weights(1, c, wexp_again)
            for i in range(4):
                low_activations(1, i)

        @block.scalar
        def _(act):
            def root(n, half):
                act.wait_ge(var_ready, 2 * n + half + 1)
                act.activation(sd[:, 4 * half:4 * half + 4], varE[:, 4 * half:4 * half + 4], ACT.Sqrt) \
                    .then_inc(sd_ready, 1)

            def drain(use, dst, src_of, scale=None):
                bank, full, free, prior = use
                act.wait_ge(full, prior + 1)
                if scale is None:
                    act.copy(dst, src_of(bank)).then_inc(free, 1)
                else:
                    act.activation(dst, src_of(bank), ACT.Copy, scale=scale).then_inc(free, 1)

            def xnT_drain(n, i):
                drain(t_use(("xnT", n, i)), xnT[:, :, 256 * i:256 * i + 256],
                      lambda b: b[:, :].rearrange("p (k n) -> p k n", k=KD))

            def split_drain(f, n, i):
                bank, full, free, prior = t_use(("xnT", n, i))
                view = bank[:, :].rearrange("p (k n) -> p k n", k=KD)
                act.wait_ge(full, prior + 1)
                cols = slice(256 * i, 256 * i + 256)
                act.copy(xraw[:, :, cols], view).then_inc(free, 1)
                act.wait_ge(free, prior + 1)
                act.copy(xhi[:, :, cols], xraw[:, :, cols]).then_inc(xhi_ready, 1)

            def high_weights(c):
                act.wait_ge(wexp_in[c], 16)
                act.copy(whi[:, c, :, :], wraw[:, c, :, :]).then_inc(whi_ready, 1)

            def ffn(f, n):
                for half in range(2):
                    for i in range(2):
                        split_drain(f, n, 2 * half + i)
                    if f == 0 and half == 0:
                        for c in range(2):
                            high_weights(c)
                    act.wait_ge(gap_ready, 2 * f + half + 1)
                    act.activation(egap[:, 4 * half:4 * half + 4], gap[:, 4 * half:4 * half + 4], ACT.Exp) \
                        .then_inc(egap_ready, 1)
                    if f == 0 and half == 0:
                        for c in range(2, CHUNKS):
                            high_weights(c)
                    if f == 1 and half == 0:
                        root(2, 1)
                    drain(t_use(("wT", f, half)), wT[:, BANK * half:BANK * (half + 1)], lambda b: b[0:E, :])

            root(0, 0)
            root(0, 1)
            ffn(0, 0)
            root(1, 0)
            for i in range(4):
                k, half = i // 2, i % 2
                drain(yr.use(("absorb_k", i)), wq[:, k, 8 * half:8 * half + 8, 0:KV],
                      lambda b: b[0:QK, :].rearrange("p (h n) -> p h n", h=8))
            for i in range(4):
                drain(yr.use(("absorb_v", i)), absV[:, 2 * i:2 * i + 2, :],
                      lambda b: b[:, :].rearrange("p (h n) -> p h n", h=2))
            for half in range(2):
                if half == 1:
                    root(1, 1)
                for i in range(2):
                    xnT_drain(1, 2 * half + i)
                drain(yr.use(("index_gate", half)), gT[:, BANK * half:BANK * (half + 1)], lambda b: b[0:IH, :])
                drain(yr.use(("latent_kv", half)), kf[:, 4 * half:4 * half + 4, :],
                      lambda b: b[:, :].rearrange("p (t n) -> p t n", t=4))
                for m in range(2):
                    drain(yr.use(("latent_q", m, half)), cpT[:, m, BANK * half:BANK * (half + 1)], lambda b: b[0:QK, :])
            for i in range(2):
                drain(tr.use(("keysT", i)), keysT[:, BANK * i:BANK * (i + 1)], lambda b: b[:, :])

            def query_copy(prior, j):
                act.wait_ge(m_full, prior + 1)
                act.copy(qtok[:, j % Q_SLOTS, :, :], M[:, 0:2 * P].rearrange("p (h n) -> p h n", h=2)).then_inc(m_free, 1)

            def queryT_drain(use, j):
                drain(use, qT[:, :, P * j:P * (j + 1)],
                      lambda b: b[:, 0:2 * P].rearrange("p (h n) -> p h n", h=2), scale=SCALE)

            for j in range(NT):
                query_copy(mr.use(("query", j))[3], j)
                if j >= 2:
                    queryT_drain(tr.use(("queryT", j - 2)), j - 2)
                if j == SEXP_AT:
                    act.wait_ge(sscore_ready, 1)
                    act.activation(sp_, ssc, ACT.Exp, bias=snm, accum_out=ssum).then_inc(sexp_ready, 1)

            def body(g):
                last = isinstance(g, int) and g == PAIRS - 1
                items = turn_items(g)
                for u in range(UNITS):
                    qt, h = u // 2, u % 2
                    for kind, args, b, prior in items[u]:
                        if kind == "probsT" and args[1] == 1:
                            probsT_drain(drain, (TB[b], t_full[b], t_free[b], prior), *args)
                    act.wait_ge(negmax_ready, UNITS * g + u + 1)
                    act.activation(probs[:, u % 4, 0:P * (qt + 1)], S[u % 2][:, 0:P * (qt + 1)], ACT.Exp,
                                   bias=negmax[:, u % 4:u % 4 + 1],
                                   accum_out=sums[:, qt // GT, qt % GT, h:h + 1]).then_inc(probs_ready, 1)
                    if h == 0 and not last:
                        query_copy(m_query(g, qt), qt)
                    for kind, args, b, prior in items[u]:
                        use = (TB[b], t_full[b], t_free[b], prior)
                        if kind == "queryT":
                            queryT_drain(use, args[0])
                        elif kind == "sumsT":
                            drain(use, rT[:, args[0], :], lambda bank: bank[:, :])

            body(0)
            with act.Fori(1, PAIRS - 1) as g:
                body(g)
            body(PAIRS - 1)
            for v in (UNITS - 2, UNITS - 1):
                probsT_drain(drain, t_use(("probsT", v, 1)), v, 1)
            drain(t_use(("sumsT", 1)), rT[:, 1, :], lambda bank: bank[:, :])
            root(2, 0)
            ffn(1, 2)

        @block.tensor
        def _(pe):
            def begin(use):
                bank, full, free, prior = use
                if not isinstance(prior, int) or prior > 0:
                    pe.wait_ge(free, prior)
                return bank

            def xnT_turn(n, half):
                for i in (2 * half, 2 * half + 1):
                    use = t_use(("xnT", n, i))
                    bank = begin(use)
                    pe.wait_ge(xn_ready, NT * n + 2 * i + 2)
                    for t in range(2):
                        for k in range(KD):
                            mm = pe.transpose(bank[:, k * 256 + t * P:k * 256 + (t + 1) * P],
                                              xn[:, 2 * i + t, k * P:(k + 1) * P], ident[:, :])
                    mm.then_inc(use[1], 1)

            def xnT_wait(n, i):
                use = t_use(("xnT", n, i))
                pe.wait_ge(use[2], use[3] + 1)

            def bias(f, i):
                use = c_use(("bias", f, i))
                bank = begin(use)
                w = t_use(("wT", f, i // 2))
                pe.wait_ge(w[2], w[3] + 1)
                for t in range(2):
                    mm = pe.matmul(bank[:, t * O:(t + 1) * O], wT[:, (2 * i + t) * P:(2 * i + t + 1) * P],
                                   bexp[:, :], start=True, stop=True)
                mm.then_inc(use[1], 1)

            def gate(f, n, half):
                use = m_use(("gate", f, half))
                bank = begin(use)
                pe.wait_ge(gate_in, 32)
                for t in range(4 * half, 4 * half + 4):
                    if t % 2 == 0:
                        xnT_wait(n, t // 2)
                    for k in range(KD):
                        mm = pe.matmul(bank[:, t * E:(t + 1) * E], xraw[:, k, t * P:(t + 1) * P], wgate[:, k, :],
                                       start=(k == 0), stop=(k == KD - 1))
                mm.then_inc(use[1], 1)

            def experts(f, t):
                for c in range(CHUNKS):
                    use = y_use(("y", f, t, c))
                    bank = begin(use)
                    if t == 0:
                        if f == 0:
                            pe.wait_ge(whi_ready, c + 1)
                        pe.wait_ge(wlo_ready, CHUNKS * f + c + 1)
                    if t % 2 == 0 and c == 0:
                        pe.wait_ge(xhi_ready, 4 * f + t // 2 + 1)
                        pe.wait_ge(xlo_ready, 4 * f + t // 2 + 1)
                    cols = slice(t * P, (t + 1) * P)
                    for k in range(KD):
                        pe.matmul(bank, xhi[:, k, cols], whi[:, c, k, :], start=(k == 0), stop=False)
                        pe.matmul(bank, xhi[:, k, cols], wlo[f][:, c, k, :], start=False, stop=False)
                        mm = pe.matmul(bank, xlo[:, k, cols], whi[:, c, k, :], start=False, stop=(k == KD - 1))
                    mm.then_inc(use[1], 1)

            def weights_turn(f, half):
                use = t_use(("wT", f, half))
                bank = begin(use)
                pe.wait_ge(wts_ready, 2 * f + half + 1)
                for tt in range(4):
                    mm = pe.transpose(bank[0:E, tt * P:(tt + 1) * P], wts[:, 4 * half + tt, :], ident[:, :])
                mm.then_inc(use[1], 1)

            def ffn(f, n):
                experts(f, 0)
                weights_turn(f, 0)
                experts(f, 1)
                xnT_turn(n, 1)
                experts(f, 2)
                gate(f, n, 1)
                bias(f, 0)
                experts(f, 3)
                experts(f, 4)
                weights_turn(f, 1)
                bias(f, 1)
                experts(f, 5)
                experts(f, 6)
                bias(f, 2)
                experts(f, 7)
                bias(f, 3)

            pe.wait_ge(ident_made, 1)
            xnT_turn(0, 0)
            gate(0, 0, 0)
            ffn(0, 0)

            pe.wait_ge(absorb_in, 32)
            for i in range(4):
                use = yr.use(("absorb_k", i))
                bank = begin(use)
                k, half = i // 2, i % 2
                for n in range(8):
                    h = 8 * half + n
                    mm = pe.matmul(bank[0:QK, n * KV:(n + 1) * KV], wqcT[:, h, k * QK:(k + 1) * QK], wkcT[:, h, :],
                                   start=True, stop=True)
                mm.then_inc(use[1], 1)
            pe.wait_ge(wo_in, 32)
            for i in range(4):
                use = yr.use(("absorb_v", i))
                bank = begin(use)
                for n in range(2):
                    for h in range(2):
                        head = 4 * i + 2 * n + h
                        mm = pe.matmul(bank[64 * h:64 * h + 64, n * O:(n + 1) * O], wvT[:, head, :], wo[:, head, :],
                                       start=True, stop=True)
                mm.then_inc(use[1], 1)

            for half in range(2):
                xnT_turn(1, half)
                cols = slice(BANK * half, BANK * (half + 1))
                xnT_wait(1, 2 * half)
                xnT_wait(1, 2 * half + 1)
                use = yr.use(("index_gate", half))
                bank = begin(use)
                if half == 0:
                    pe.wait_ge(index_in, 16 * 6)
                for k in range(KD):
                    mm = pe.matmul(bank[0:IH, :], widx_gate[:, k, :], xnT[:, k, cols], start=(k == 0), stop=(k == KD - 1))
                mm.then_inc(use[1], 1)
                use = yr.use(("latent_kv", half))
                bank = begin(use)
                if half == 0:
                    pe.wait_ge(latent_in, 16 * 4)
                for t in range(4):
                    for k in range(KD):
                        mm = pe.matmul(bank[:, t * P:(t + 1) * P], xnT[:, k, (4 * half + t) * P:(4 * half + t + 1) * P],
                                       wkv[:, k, :], start=(k == 0), stop=(k == KD - 1))
                mm.then_inc(use[1], 1)
                for m in range(2):
                    use = yr.use(("latent_q", m, half))
                    bank = begin(use)
                    for k in range(KD):
                        mm = pe.matmul(bank[0:QK, :], wcp[:, k, m * QK:(m + 1) * QK], xnT[:, k, cols],
                                       start=(k == 0), stop=(k == KD - 1))
                    mm.then_inc(use[1], 1)
            for i in range(2):
                use = tr.use(("keysT", i))
                bank = begin(use)
                pe.wait_ge(key_roped, i + 1)
                for t in range(4):
                    mm = pe.transpose(bank[:, t * P:(t + 1) * P], kf[:, 4 * i + t, :], ident[:, :])
                mm.then_inc(use[1], 1)

            def index_step(name):
                use = cr.use((name,))
                return use, begin(use)

            def sel_onehot():
                use, bank = index_step("onehot")
                pe.wait_ge(hot_ready, 1)
                for t in range(NT):
                    mm = pe.transpose(bank[:, t * SEL:(t + 1) * SEL], hotT[:, t * P:(t + 1) * P], ident[0:SEL, 0:SEL])
                mm.then_inc(use[1], 1)

            def sel_rows():
                use, bank = index_step("rows")
                for k in range(KD):
                    for t in range(NT):
                        mm = pe.matmul(bank[:, k * SEL:(k + 1) * SEL], xn[:, t, k * P:(k + 1) * P], onehot[:, t, :],
                                       start=(t == 0), stop=(t == NT - 1))
                mm.then_inc(use[1], 1)

            def sel_states():
                use, bank = index_step("selected")
                for h in range(IH):
                    for k in range(KD):
                        mm = pe.matmul(bank[:, h * TOPK:(h + 1) * TOPK], widx[:, k, h * ID:(h + 1) * ID],
                                       rowsT[:, k, h * TOPK:(h + 1) * TOPK], start=(k == 0), stop=(k == KD - 1))
                mm.then_inc(use[1], 1)

            def sel_qkv():
                use, bank = index_step("sqkv")
                for w in range(2):
                    pe.matmul(bank[:, w * SEL:(w + 1) * SEL], ws3[:, w, :], selT, start=True, stop=True)
                pe.matmul(bank[0:SEL, P:2 * P], selT, ws3[:, 2, :], start=True, stop=True).then_inc(use[1], 1)

            def sel_scores():
                use, bank = index_step("sscores")
                pe.matmul(bank[0:SEL, 0:SEL], sqkT[:, 0, :], sqkT[:, 1, :], start=True, stop=True).then_inc(use[1], 1)

            def sel_mean():
                use, bank = index_step("smean")
                pe.wait_ge(sprob_ready, 1)
                pe.wait_ge(masks_made, 5)
                pe.matmul(bank[0:SEL, 0:IH], sprob, groups, start=True, stop=True).then_inc(use[1], 1)

            def sel_out():
                use, bank = index_step("sout")
                pe.matmul(bank[:, 0:IH], sv, smean, start=True, stop=True).then_inc(use[1], 1)

            def sel_io():
                use, bank = index_step("io")
                pe.matmul(bank[:, 0:IH], ws3[:, 3, :], soutT, start=True, stop=True).then_inc(use[1], 1)

            def sel_row():
                use, bank = index_step("io_row")
                pe.wait_ge(wosum_ready, 1)
                for h in range(IH):
                    mm = pe.matmul(bank[0:1, 0:O], ioT[:, h:h + 1], wosum[:, h, :], start=(h == 0), stop=(h == IH - 1))
                mm.then_inc(use[1], 1)

            def sel_all():
                use, bank = index_step("io_all")
                pe.matmul(bank[:, 0:O], ones[0:1, :], iorow[:, :], start=True, stop=True).then_inc(use[1], 1)

            def query(prior, pair, j):
                pe.wait_ge(m_free, prior)
                cols = wq[:, :, :, :].rearrange("p k h n -> p k (h n)")
                for k in range(2):
                    mm = pe.matmul(M[:, 0:2 * P], cpT[:, k, j * P:(j + 1) * P],
                                   cols[:, k, bass.ds(pair * 2 * P, 2 * P)], start=(k == 0), stop=(k == 1))
                mm.then_inc(m_full, 1)

            def query_turn(use, n, j):
                bank = begin(use)
                pe.wait_ge(query_roped, n + 1)
                for h in range(2):
                    mm = pe.transpose(bank[:, h * P:(h + 1) * P], qtok[:, j % Q_SLOTS, h, :], ident[:, :])
                mm.then_inc(use[1], 1)

            for half in range(2):
                for m in range(2):
                    use = yr.use(("latent_q", m, half))
                    pe.wait_ge(use[2], use[3] + 1)
            index_steps = (sel_onehot, sel_rows, sel_states, sel_qkv, sel_scores, sel_mean, sel_out, sel_io)
            for j in range(NT):
                query(mr.use(("query", j))[3], 0, j)
                if j >= 2:
                    query_turn(tr.use(("queryT", j - 2)), j - 2, j - 2)
                index_steps[j]()
            sel_row()
            sel_all()

            def scores(g, u):
                qt, h = u // 2, u % 2
                w = P * (qt + 1)
                s = S[u % 2]
                for c in range(0, w, BANK):
                    n = min(BANK, w - c)
                    mm = pe.matmul(s[:, c:c + n], qT[:, h, P * qt:P * (qt + 1)], keysT[:, c:c + n],
                                   start=True,
                                   stop=(u >= MASK_ON_DVE or c + n < w))
                if u >= MASK_ON_DVE:
                    mm.then_inc(scores_ready, 1)
                    return
                pe.matmul(s[:, P * qt:w], identb[:, :], causal[:, :], start=False, stop=True) \
                    .then_inc(scores_ready, 1)

            def probs_turn(use, v, c):
                bank = begin(use)
                n = min(GT, tiles_of(v) - GT * c)
                for k in range(n):
                    kt = GT * c + k
                    mm = pe.transpose(bank[:, k * P:(k + 1) * P], probs[:, v % 4, kt * P:(kt + 1) * P], ident[:, :])
                mm.then_inc(use[1], 1)

            def sums_turn(use, n):
                bank = begin(use)
                pe.wait_ge(rwide_ready, n + 1)
                for t in range(GT):
                    mm = pe.transpose(bank[:, t * P:(t + 1) * P], rwide[:, t, :, :].rearrange("p h n -> p (h n)"), ident[:, :])
                mm.then_inc(use[1], 1)

            def pv(group, kt, prior):
                if kt == 0:
                    pe.wait_ge(c_free, prior)
                pT, kts = (pT0, GT) if group == 0 else (pT1, NT)
                q0 = max(0, kt - GT * group) * P
                for h in range(2):
                    mm = pe.matmul(C[64 * h:64 * h + 64, q0:BANK], kf[:, kt, 0:KV], pT[:, h, kt, q0:BANK],
                                   start=(kt == 0), stop=(kt == kts - 1))
                if kt == kts - 1:
                    mm.then_inc(c_full, 1)

            for i in range(4):
                pe.wait_ge(y_free[i], y_base)
            pe.wait_ge(tr.use(("keysT", 0))[2], tr.use(("keysT", 0))[3] + 1)
            pe.wait_ge(tr.use(("keysT", 1))[2], tr.use(("keysT", 1))[3] + 1)
            pe.wait_ge(masks_made, 5)

            def turn(g, kind, args, b, prior):
                use = (TB[b], t_full[b], t_free[b], prior)
                if kind == "probsT":
                    probs_turn(use, *args)
                elif kind == "queryT":
                    j = args[0]
                    query_turn(use, NT * g + j if j >= Q_LATE else NT * (g + 1) + j, j)
                else:
                    sums_turn(use, 2 * g - 1 if args[0] == 1 else 2 * g)

            def body(g):
                first, last = isinstance(g, int) and g == 0, isinstance(g, int) and g == PAIRS - 1
                items = turn_items(g)
                for u in range(UNITS):
                    if not first or u >= 2:
                        pe.wait_ge(probs_ready, UNITS * g + u - 1)
                    probs_items = [it for it in items[u] if it[0] == "probsT"]
                    for item in probs_items[:1]:
                        turn(g, *item)
                    scores(g, u)
                    if not first and PV_AT[1] <= u < PV_AT[1] + NT:
                        pv(1, u - PV_AT[1], c_group(g - 1, 1))
                    if u >= PV_AT[0]:
                        pv(0, u - PV_AT[0], c_group(g, 0))
                    if not first and u < PV0_LATE:
                        pv(0, u + GT - PV0_LATE, c_group(g - 1, 0))
                    for item in probs_items[1:]:
                        turn(g, *item)
                    if u % 2 == 0 and not last:
                        query(m_query(g, u // 2), g + 1, u // 2)
                    for item in items[u]:
                        if item[0] != "probsT":
                            turn(g, *item)

            body(0)
            with pe.Fori(1, PAIRS - 1) as g:
                body(g)
            body(PAIRS - 1)

            def project(t):
                use = y_use(("project", t))
                bank = begin(use)
                for g in range(PAIRS):
                    mm = pe.matmul(bank[:, 0:O], ctxT[:, g, t * P:(t + 1) * P], absV[:, g, :],
                                   start=(g == 0), stop=(g == PAIRS - 1))
                mm.then_inc(use[1], 1)

            pe.wait_ge(probs_ready, UNITS * PAIRS)
            for v in (UNITS - 2, UNITS - 1):
                for c in range(chunks_of(v)):
                    probs_turn(t_use(("probsT", v, c)), v, c)
            for kt in range(GT - PV0_LATE, GT):
                pv(0, kt, c_group(PAIRS - 1, 0))
            pe.wait_ge(c_free, c_group(PAIRS - 1, 0) + 1)
            for t in range(GT):
                project(t)
            sums_turn(t_use(("sumsT", 1)), 2 * PAIRS - 1)
            for c in range(2):
                use = t_use(("probsT", UNITS - 1, c))
                pe.wait_ge(use[2], use[3] + 1)
            for kt in range(NT):
                pv(1, kt, c_group(PAIRS - 1, 1))
            xnT_turn(2, 0)
            pe.wait_ge(c_free, c_group(PAIRS - 1, 1) + 1)
            for t in range(GT, NT):
                project(t)
            gate(1, 2, 0)
            ffn(1, 2)

        @block.vector
        def _(dve):
            steps = [0]

            def settle(ins):
                ins.then_inc(dve_step, 1)
                steps[0] += 1
                dve.wait_ge(dve_step, steps[0])

            def tick(ins):
                ins.then_inc(dve_step, 1)
                steps[0] += 1

            def norm_stats(n, half):
                ts = range(4 * half, 4 * half + 4)
                hs = slice(4 * half, 4 * half + 4)
                for t in ts:
                    if n == 0 and t % 2 == 0:
                        dve.wait_ge(x_in[t // 2], 16)
                    tick(dve.bn_stats(stats[:, t, :], x[:, t, :]))
                dve.wait_ge(dve_step, steps[0])
                for t in ts:
                    tick(dve.bn_aggr(mv[:, t, :], stats[:, t, :]))
                dve.wait_ge(dve_step, steps[0])
                dve.tensor_scalar(varE[:, hs], mv[:, hs, 1], EPS, None, ALU.add).then_inc(var_ready, 1)

            def norm_apply(n, half):
                hs = slice(4 * half, 4 * half + 4)
                dve.wait_ge(sd_ready, 2 * n + half + 1)
                settle(dve.reciprocal(rs0[:, hs], sd[:, hs]))
                settle(dve.scalar_tensor_tensor(out=rs0[:, hs], in0=varE[:, hs], scalar=0.5, in1=rs0[:, hs],
                                                op0=ALU.mult, op1=ALU.mult))
                settle(dve.scalar_tensor_tensor(out=rs0[:, hs], in0=sd[:, hs], scalar=0.5, in1=rs0[:, hs],
                                                op0=ALU.mult, op1=ALU.add))
                settle(dve.reciprocal(rstd[:, hs], rs0[:, hs]))
                for t in range(4 * half, 4 * half + 4):
                    dve.tensor_scalar(xn[:, t, :], x[:, t, :], mv[:, t, 0:1], rstd[:, t:t + 1],
                                      ALU.subtract, ALU.mult).then_inc(xn_ready, 1)

            def route(f, half):
                ts = range(4 * half, 4 * half + 4)
                hs = slice(4 * half, 4 * half + 4)
                n = 2 * f + half + 1
                bank, full, free, prior = m_use(("gate", f, half))
                dve.wait_ge(full, prior + 1)
                dve.tensor_copy(logits[:, hs, :], bank[:, 32 * half:32 * half + 32].rearrange("p (t e) -> p t e", e=E)) \
                    .then_inc(free, 1)
                dve.wait_ge(free, prior + 1)
                for t in ts:
                    tick(dve.max(top[:, t, :], logits[:, t, :]))
                dve.wait_ge(dve_step, steps[0])
                dve.tensor_tensor(gap[:, hs], top[:, hs, 1], top[:, hs, 0], ALU.subtract).then_inc(gap_ready, 1)
                for t in ts:
                    tick(dve.max_index(topi[:, t, :], top[:, t, :], logits[:, t, :]))
                dve.wait_ge(dve_step, steps[0])
                settle(dve.tensor_copy(topf[:, hs, :], topi[:, hs, 0:2]))
                if n == 1:
                    dve.wait_ge(iotas_made, 1)
                for k in range(2):
                    tick(dve.tensor_tensor(hot[:, k, hs, :], iota8[:, hs, :],
                                           topf[:, hs, k:k + 1].to_broadcast([P, 4, E]), ALU.is_equal))
                dve.wait_ge(egap_ready, n)
                settle(dve.tensor_scalar(w2[:, hs], egap[:, hs], 2.0, 2.0, ALU.mult, ALU.add))
                settle(dve.reciprocal(w1[:, hs], w2[:, hs]))
                settle(dve.tensor_tensor(w2[:, hs], w1[:, hs], egap[:, hs], ALU.mult))
                for k, w in enumerate((w1, w2)):
                    tick(dve.tensor_tensor(hot[:, k, hs, :], hot[:, k, hs, :],
                                           w[:, hs].unsqueeze(2).to_broadcast([P, 4, E]), ALU.mult))
                dve.wait_ge(dve_step, steps[0])
                dve.tensor_tensor(wts[:, hs, :], hot[:, 0, hs, :], hot[:, 1, hs, :], ALU.add).then_inc(wts_ready, 1)
                dve.wait_ge(wts_ready, n)

            def combine(f, t):
                for c in range(CHUNKS):
                    bank, full, free, prior = y_use(("y", f, t, c))
                    dve.wait_ge(full, prior + 1)
                    for e in range(2):
                        ins = dve.scalar_tensor_tensor(out=x[:, t, :], in0=bank[:, e * O:(e + 1) * O],
                                                       scalar=wts[:, t, 2 * c + e:2 * c + e + 1], in1=x[:, t, :],
                                                       op0=ALU.mult, op1=ALU.add)
                        if e == 0:
                            settle(ins)
                        else:
                            ins.then_inc(free, 1)
                            dve.wait_ge(free, prior + 1)

            def add_bias(f, i):
                bank, full, free, prior = c_use(("bias", f, i))
                dve.wait_ge(full, prior + 1)
                ins = dve.tensor_tensor(x[:, 2 * i:2 * i + 2, :], bank[:, :].rearrange("p (t n) -> p t n", t=2),
                                        x[:, 2 * i:2 * i + 2, :], ALU.add)
                ins.then_inc(free, 1)
                dve.wait_ge(free, prior + 1)

            norm_stats(0, 0)
            norm_stats(0, 1)
            norm_apply(0, 0)
            norm_apply(0, 1)
            route(0, 0)
            for t in range(3):
                combine(0, t)
            add_bias(0, 0)
            route(0, 1)
            combine(0, 3)
            combine(0, 4)
            add_bias(0, 1)
            norm_stats(1, 0)
            combine(0, 5)
            combine(0, 6)
            add_bias(0, 2)
            combine(0, 7)
            add_bias(0, 3)
            norm_stats(1, 1)
            norm_apply(1, 0)
            norm_apply(1, 1)

            def take(name, dst, src):
                bank, full, free, prior = cr.use((name,))
                dve.wait_ge(full, prior + 1)
                dve.tensor_copy(dst, src(bank)).then_inc(free, 1)

            for i in range(2):
                use = yr.use(("index_gate", i))
                dve.wait_ge(use[2], use[3] + 1)
            settle(dve.max(gtop, gT))
            settle(dve.max_index(gidx, gtop, gT))
            dve.tensor_copy(gidf, gidx).then_inc(index_listed, 1)
            dve.wait_ge(index_spread, 16)
            dve.wait_ge(iotas_made, 2)
            dve.tensor_scalar(hotT, iotaT, idxp, None, ALU.is_equal).then_inc(hot_ready, 1)
            take("onehot", onehot, lambda b: b[:, :].rearrange("p (t s) -> p t s", t=NT))
            take("rows", rowsT, lambda b: b[:, 0:KD * SEL].rearrange("p (k s) -> p k s", k=KD))
            take("selected", selT, lambda b: b[:, 0:SEL])
            bank, full, free, prior = cr.use(("sqkv",))
            dve.wait_ge(full, prior + 1)
            tick(dve.tensor_copy(sv, bank[0:SEL, P:2 * P]))
            dve.tensor_copy(sqkT, bank[:, 0:2 * SEL].rearrange("p (w s) -> p w s", w=2)).then_inc(free, 1)
            bank, full, free, prior = cr.use(("sscores",))
            dve.wait_ge(full, prior + 1)
            dve.wait_ge(masks_made, 5)
            dve.scalar_tensor_tensor(out=ssc, in0=bank[0:SEL, 0:SEL], scalar=1.0 / float(np.sqrt(ID)), in1=blockmask,
                                     op0=ALU.mult, op1=ALU.add).then_inc(free, 1)
            dve.wait_ge(free, prior + 1)
            dve.tensor_reduce(snm, ssc, AX.X, ALU.max, negate=True).then_inc(sscore_ready, 1)
            dve.wait_ge(sexp_ready, 1)
            settle(dve.reciprocal(srs, ssum))
            dve.tensor_scalar(sprob, sp_, srs, None, ALU.mult).then_inc(sprob_ready, 1)
            take("smean", smean, lambda b: b[0:SEL, 0:IH])
            take("sout", soutT, lambda b: b[:, 0:IH])
            take("io", ioT, lambda b: b[:, 0:IH])
            take("io_row", iorow[:, :], lambda b: b[0:1, 0:O])
            bank, full, free, prior = cr.use(("io_all",))
            dve.wait_ge(full, prior + 1)
            dve.tensor_tensor(x[:, :, :], x[:, :, :], bank[:, 0:O].unsqueeze(1).to_broadcast([P, NT, O]), ALU.add) \
                .then_inc(free, 1)

            def drain(use, dst, src_of):
                bank, full, free, prior = use
                dve.wait_ge(full, prior + 1)
                dve.tensor_copy(dst, src_of(bank)).then_inc(free, 1)

            def group_sums(group, n):
                dve.wait_ge(probs_ready, n)
                dve.reciprocal(rsum[:, group, :, :], sums[:, group, :, :]).then_inc(rsum_ready, 1)

            def context(g, group, prior, r_use):
                dve.wait_ge(c_full, prior + 1)
                dve.wait_ge(r_use[2], r_use[3] + 1)
                flat = ctxT[:, :, :].rearrange("p g n -> p (g n)")
                dve.tensor_tensor(flat[:, bass.ds(g * T + group * BANK, BANK)], C[:, :], rT[:, group, :], ALU.mult) \
                    .then_inc(c_free, 1)

            def sums_use(items, group):
                (kind, args, b, prior), = [i for i in items[R_AT[group]] if i[0] == "sumsT"]
                return TB[b], t_full[b], t_free[b], prior

            def body(g):
                first = isinstance(g, int) and g == 0
                items = turn_items(g)
                for u in range(UNITS):
                    qt = u // 2
                    for kind, args, b, prior in items[u]:
                        if kind == "probsT" and args[1] == 0:
                            probsT_drain(drain, (TB[b], t_full[b], t_free[b], prior), *args)
                    dve.wait_ge(scores_ready, UNITS * g + u + 1)
                    if u >= MASK_ON_DVE:
                        diagonal = S[u % 2][:, P * qt:P * (qt + 1)]
                        dve.tensor_tensor(diagonal, diagonal, causal[:, :], ALU.add).then_inc(masked, 1)
                        dve.wait_ge(masked, (UNITS - MASK_ON_DVE) * g + u - MASK_ON_DVE + 1)
                    dve.tensor_reduce(negmax[:, u % 4:u % 4 + 1], S[u % 2][:, 0:P * (qt + 1)], AX.X, ALU.max,
                                      negate=True).then_inc(negmax_ready, 1)
                    if u == PV0_LATE and not first:
                        b0 = sums_before(g)
                        context(g - 1, 0, c_group(g - 1, 0), b0)
                    if u == 1 and not first:
                        group_sums(1, UNITS * g)
                    if u == 9:
                        group_sums(0, UNITS * g + 8)
                    if u == PV_AT[1] + NT and not first:
                        context(g - 1, 1, c_group(g - 1, 1), sums_use(items, 1))

            def sums_before(g):
                if isinstance(g, int):
                    return sums_use(turn_items(g - 1), 0)
                return sums_use(turn_items(g - 1), 0)

            body(0)
            with dve.Fori(1, PAIRS - 1) as g:
                body(g)
            body(PAIRS - 1)
            group_sums(1, UNITS * PAIRS)
            for v in (UNITS - 2, UNITS - 1):
                probsT_drain(drain, t_use(("probsT", v, 0)), v, 0)
            context(PAIRS - 1, 0, c_group(PAIRS - 1, 0), sums_before(PAIRS))

            def residual(t):
                bank, full, free, prior = y_use(("project", t))
                dve.wait_ge(full, prior + 1)
                ins = dve.tensor_tensor(x[:, t, :], bank[:, 0:O], x[:, t, :], ALU.add)
                ins.then_inc(free, 1)
                dve.wait_ge(free, prior + 1)

            for t in range(GT):
                residual(t)
            norm_stats(2, 0)
            norm_apply(2, 0)
            last_r = t_use(("sumsT", 1))
            context(PAIRS - 1, 1, c_group(PAIRS - 1, 1), last_r)
            for t in range(GT, NT):
                residual(t)
            norm_stats(2, 1)
            route(1, 0)
            norm_apply(2, 1)
            for t in range(3):
                combine(1, t)
            add_bias(1, 0)
            route(1, 1)
            combine(1, 3)
            combine(1, 4)
            add_bias(1, 1)
            combine(1, 5)
            combine(1, 6)
            add_bias(1, 2)
            combine(1, 7)
            add_bias(1, 3)


def kernel(L0_attn_x, L0_attn_W_c, L0_attn_W_cp, L0_attn_W_qc, L0_attn_W_qr, L0_attn_W_kc, L0_attn_W_kr, L0_attn_W_v,
           L0_attn_W_o, L0_attn_W_idx, L0_attn_W_gate, L0_attn_W_sq, L0_attn_W_sk, L0_attn_W_sv, L0_attn_W_iout,
           L0_ffn_gate_w, L0_ffn_expert_w, L0_ffn_expert_b):
    import concourse.bacc as bacc
    from concourse.bass_utils import run_bass_kernel_spmd

    halves = np.concatenate([np.arange(0, DR, 2), np.arange(1, DR, 2)])
    inv = 1.0 / 10000.0 ** (np.arange(0, DR, 2)[:DR // 2].astype(np.float32) / DR)
    freqs = np.outer(np.arange(T, dtype=np.float32), inv)
    cos, sin = np.cos(freqs).astype(np.float32), np.sin(freqs).astype(np.float32)

    def np_(v):
        return np.asarray(v)

    def tiles(v, p):
        v = np_(v)
        return v.reshape(v.shape[0] // p, p, -1).transpose(1, 0, 2)

    data = {
        "x": np_(L0_attn_x).reshape(T, D),
        "gate_w": tiles(np_(L0_ffn_gate_w).T, P),
        "expert_b": np_(L0_ffn_expert_b),
        "expert_w": np_(L0_ffn_expert_w).reshape(CHUNKS, 2, O, KD, P).transpose(4, 0, 3, 1, 2).reshape(P, CHUNKS, KD, 2 * O),
        "W_qc": np_(L0_attn_W_qc).reshape(QL, NH, DK).transpose(2, 1, 0),
        "W_kc": np_(L0_attn_W_kc).reshape(KV, NH, DK).transpose(2, 1, 0),
        "W_v": np_(L0_attn_W_v).reshape(KV, NH, DV).transpose(2, 1, 0),
        "W_o": np_(L0_attn_W_o).reshape(NH, DV, D).transpose(1, 0, 2),
        "W_qr": np_(L0_attn_W_qr).reshape(2, QK, NH, DR)[..., halves].transpose(1, 0, 2, 3),
        "W_cp": tiles(L0_attn_W_cp, P),
        "W_c": tiles(L0_attn_W_c, P),
        "W_kr": tiles(np_(L0_attn_W_kr)[:, halves], P),
        "cos": tiles(np.concatenate([cos, cos], axis=1), P),
        "sin": tiles(np.concatenate([-sin, sin], axis=1), P),
        "W_idx": tiles(L0_attn_W_idx, P),
        "W_gate": tiles(L0_attn_W_gate, P),
        "W_sq": np_(L0_attn_W_sq),
        "W_sk": np_(L0_attn_W_sk),
        "W_sv": np_(L0_attn_W_sv),
        "W_iout": np_(L0_attn_W_iout)[:, 0:DV],
    }
    nc = bacc.Bacc("TRN2", target_bir_lowering=False, num_devices=1)
    arrays, a = {}, {}
    for name, v in data.items():
        v = np.ascontiguousarray(v)
        arrays[f"in_{name}"] = v
        a[name] = nc.dram_tensor(f"in_{name}", v.shape, mybir.dt.from_np(v.dtype), kind="ExternalInput").ap()
    out = nc.dram_tensor("out", (T, D), F32, kind="ExternalOutput").ap()
    build(nc, a, out)
    r = run_bass_kernel_spmd(nc, [arrays], core_ids=[0])
    return r.results[0]["out"].reshape(1, T, D)
```

```python
import numpy as np
import concourse.bass as bass
from concourse import mybir
from contextlib import ExitStack

F32 = mybir.dt.float32
F32R = mybir.dt.float32r
BF16 = mybir.dt.bfloat16
U32 = mybir.dt.uint32
ALU = mybir.AluOpType
ACT = mybir.ActivationFunctionType
AX = mybir.AxisListType

P = 128
T, D = 1024, 256
NT, KD = T // P, D // P
E, O = 8, 256
CHUNKS = E // 2
NH, DK, DR, DV = 16, 128, 64, 128
KV, QL = 64, 192
QA, QB = P, QL - P
assert 2 * QB == P
PAIRS = NH // 2
IH, ID, TOPK = 8, 128, 8
SEL = IH * TOPK
GT = 4
SCALE = 1.0 / float(np.sqrt(DK + DR))
EPS = 1e-5
MASK_ON_DVE = 4
MASKED = -1e30
BANK = 512


class Ring:

    def __init__(self, banks, full, free, order):
        self.banks, self.full, self.free = banks, full, free
        self.at = {key: i for i, key in enumerate(order)}
        self.n = len(order)

    def use(self, key):
        i = self.at[key]
        b = i % len(self.banks)
        return self.banks[b], self.full[b], self.free[b], i // len(self.banks)


WARM_UP = 14

UNITS = 2 * NT
LAG = 3
Q_OWN = {0: 0, 2: 1}
Q_NEXT = {9: 0, 11: 1}
SPLIT_AT = 7
HI_AT = {4: 0, 6: 1}
LO_AT = {5: 0, 7: 1}
EDGE_AT = UNITS - 2
INDEX_AT = {"selected": 0, "sqkv": 1, "sscores": 2, "smean": 4, "sout": 5, "io": 6, "io_row": 7, "io_all": 8}
VECTOR_DRAINS = (1,)
R_AT = {1: 6, 0: 13}
PV_AT = {1: {4: (0,), 5: (1,), 6: (2,), 7: (3,), 8: (4,), 9: (5,), 10: (6, 7)},
         0: {12: (0,), 13: (1,), 14: (2,), 15: (3,)}}
CONTEXT_AT = {1: 11, 0: 0}

Y_ORDER = [("y", 0, t, c) for t in range(NT) for c in range(CHUNKS)] \
    + [("absorb_k", i) for i in range(4)] + [("index_gate", 0)] + [("absorb_v", i) for i in range(4)] \
    + [("latent_kv", 0), ("index_gate", 1), ("latent_kv", 1)] \
    + [("latent_q", m, half) for half in range(2) for m in range(2)]
Y_TAIL = [("project", t) for t in range(NT)] \
    + [("y", 1, t, c) for t in range(NT) for c in range(CHUNKS)]
def ffn_turns(f, n):
    return [("xnT", n, 0), ("xnT", n, 1), ("wT", f, 0), ("xnT", n, 2), ("xnT", n, 3), ("wT", f, 1)]


T_ORDER = ffn_turns(0, 0) + [("xnT", 1, i) for i in range(4)] + [("values",)]
M_ORDER = [("gate", 0, 0), ("gate", 0, 1)] + [("query", h) for h in range(2)]
C_ORDER = [("bias", 0, i) for i in range(4)] \
    + [(s,) for s in ("onehot", "rows", "selected", "sqkv", "sscores", "smean", "sout", "io", "io_row", "io_all")]

def tiles_of(v):
    return v // 2 + 1


def chunks_of(v):
    return (tiles_of(v) + GT - 1) // GT


def loop_items():
    items = []
    for u in range(UNITS):
        v = (u - LAG) % UNITS
        items += [(u, "probsT", (v, c), u < LAG) for c in range(chunks_of(v))]
        for group, at in R_AT.items():
            if at == u:
                items.append((u, "sumsT", (group,), group == 1))
    return items


LOOP_ITEMS = loop_items()
assert len(LOOP_ITEMS) % 2 == 0


def turn_items(g, pair_count=PAIRS):
    first, last = isinstance(g, int) and g == 0, isinstance(g, int) and g == pair_count - 1
    base = len(T_ORDER)
    before = [len([i for i in range(base) if i % 2 == b]) for b in range(2)]
    missing = [len([1 for n, it in enumerate(LOOP_ITEMS) if it[3] and (base + n) % 2 == b]) for b in range(2)]
    count, out = [0, 0], {u: [] for u in range(UNITS)}
    for n, (u, kind, args, needs_earlier) in enumerate(LOOP_ITEMS):
        if first and needs_earlier:
            continue
        b = (base + n) % 2
        start = before[b] if first else before[b] - missing[b] + g * (len(LOOP_ITEMS) // 2)
        out[u].append((kind, args, b, start + count[b]))
        count[b] += 1
    return out


def turn_tail():
    last = turn_items(PAIRS - 1)
    seen = [0, 0]
    for items in last.values():
        for _, _, b, prior in items:
            seen[b] = prior + 1
    order = [("probsT", v, c) for v in range(UNITS - LAG, UNITS) for c in range(chunks_of(v))] \
        + [("sumsT", 1)] + ffn_turns(1, 2)
    out = {}
    for i, key in enumerate(order):
        out[key] = (i % 2, seen[i % 2])
        seen[i % 2] += 1
    return out


def build(nc, a, out):
    ctx = ExitStack()
    with ctx:
        def sb(name, shape, dt=F32):
            return ctx.enter_context(nc.sbuf_tensor(name, shape, dt))

        def sb_over(name, shape, base, dt=F32R):
            return nc.alloc_sbuf_tensor_at(name, shape, dt, offset=base)

        def base():
            return (nc.sbuf_base + 31) // 32 * 32

        def sem(name):
            return ctx.enter_context(nc.semaphore(name))

        x = sb("x", [P, NT, D])
        whi_base = base()
        whi = sb("whi", [P, CHUNKS, KD, 2 * O], F32R)
        wgate = sb("wgate", [P, KD, E])
        bexp = sb("bexp", [E, O])
        wts = sb("wts", [P, NT, E])
        rows = sb("rows", [P, T])
        wT = rows[0:E, :]
        cosT = rows[KV:P, :]
        stats = sb("stats", [P, NT, 6])
        mv = sb("mv", [P, NT, 2])
        varE = sb("varE", [P, NT])
        sd = sb("sd", [P, NT])
        rs0 = sb("rs0", [P, NT])
        rstd = sb("rstd", [P, NT])
        logits = sb("logits", [P, NT, E])
        top = sb("top", [P, NT, 8])
        topi = sb("topi", [P, NT, 8], U32)
        topf = sb("topf", [P, NT, 2])
        gap = sb("gap", [P, NT])
        egap = sb("egap", [P, NT])
        w1 = sb("w1", [P, NT])
        w2 = sb("w2", [P, NT])
        hot = sb("hot", [P, 2, NT, E])
        iota8 = sb("iota8", [P, NT, E])

        wq_room = sb("wq_room", [P, 2 * NH * P])
        wq = wq_room[:, :].rearrange("p (k h n) -> p k h n", k=2, h=NH)
        wraw = wq_room[:, :].rearrange("p (c k n) -> p c k n", c=CHUNKS, k=KD)
        wcp = sb("wcp", [P, KD, 2 * P])
        wkv = sb("wkv", [P, KD, P])
        widx_gate = sb("widx_gate", [P, KD, IH])
        cpT_base = base()
        cpT_room = sb("cpT_room", [P, 2, T])
        xraw = cpT_room[:, :, :]
        cp_hi = sb_over("cp_hi", [P, T], cpT_base)
        cp_lo = sb_over("cp_lo", [P, T], cpT_base + T * 4)
        cp_b = sb("cp_b", [P, T], F32R)
        ws_hi = sb("ws_hi", [P, 2, 2 * P], F32R)
        ws_lo = sb("ws_lo", [P, 2, 2 * P], F32R)
        values = sb("values", [P, NT, KV])
        keysT = sb("keysT", [P, T])
        swapped = sb("swapped", [P, 2, BANK])
        turned = sb("turned", [P, BANK])[KV:P, :]
        sinT = sb("sinT", [P, T])[KV:P, :]
        qT_base = base()
        qT = sb("qT", [P, 2, T])
        probs_base = base()
        probs = sb("probs", [P, 4, T])
        xn = probs[:, 0:2, :].rearrange("p a (t n) -> p (a t) n", n=D)
        xnT = probs[:, 2:4, :]
        k_hi = sb_over("k_hi", [P, T], whi_base)
        k_lo = sb_over("k_lo", [P, T], whi_base + T * 4)
        q_hi = sb_over("q_hi", [P, 2, BANK], whi_base + 2 * T * 4)
        q_lo = sb_over("q_lo", [P, 2, BANK], whi_base + 3 * T * 4)
        e_hi = sb("e_hi", [P, 2, P], F32R)
        e_lo = sb("e_lo", [P, 2, P], F32R)
        xhi = sb_over("xhi", [P, KD, T], probs_base + 2 * T * 4)
        xlo = sb_over("xlo", [P, KD, T], qT_base)
        pT0_base = base()
        pT0 = sb("pT0", [P, 2, GT, BANK])
        pT1 = sb("pT1", [P, 2, NT, BANK])
        ctxT_base = base()
        ctxT = sb("ctxT", [P, PAIRS, T])
        absV = sb("absV", [P, PAIRS, O])
        negmax = sb("negmax", [P, 4])
        sums = sb("sums", [P, 2, GT, 2])
        rsum = sb("rsum", [P, 2, GT, 2])
        rwide = sb("rwide", [P, GT, 2, 64])
        rT = sb("rT", [P, 2, BANK])
        ident = sb("ident", [P, P])
        identb = sb("identb", [P, P], BF16)
        causal = sb("causal", [P, P], BF16)
        ones = sb("ones", [P, P])
        iorow = sb("iorow", [1, O])

        early1 = pT1[:, :, :, :].rearrange("p h k n -> p (h k n)")
        wlo = [sb_over(f"wlo{f}", [P, CHUNKS, KD, 2 * O], at) for f, at in enumerate((ctxT_base, pT0_base))]
        wo = early1[:, 0:4096].rearrange("p (h n) -> p h n", h=NH)
        wvT = early1[:, 4096:5120].rearrange("p (h n) -> p h n", h=NH)
        wkcT = early1[:, 5120:6144].rearrange("p (h n) -> p h n", h=NH)
        wosum = early1[:, 6144:8192].rearrange("p (h n) -> p h n", h=IH)
        early0 = pT0[:, :, :, :].rearrange("p h k n -> p (h k n)")
        wqcT = early0[:, 0:4096].rearrange("p (h n) -> p h n", h=NH)
        ws3 = ctxT[:, :, :].rearrange("p g n -> p (g n)")[:, 6400:6912].rearrange("p (w n) -> p w n", w=4)
        early2 = ctxT[:, :, :].rearrange("p g n -> p (g n)")
        widx = early2[:, 0:2048].rearrange("p (k n) -> p k n", k=KD)
        iotaT = early2[0:SEL, 2048:3072]
        hotT = early2[0:SEL, 3072:4096]
        onehot = early2[:, 4096:4608].rearrange("p (t s) -> p t s", t=NT)
        gT = early2[0:IH, 4608:5632]
        rowsT = early2[:, 5632:5760].rearrange("p (k s) -> p k s", k=KD)
        selT = early2[:, 5760:5824]
        sqkT = early2[:, 5824:5952].rearrange("p (w s) -> p w s", w=2)
        sv = early2[0:SEL, 5952:6080]
        blockmask = early2[0:SEL, 6080:6144]
        groups = early2[0:SEL, 6144:6152]
        ssc = early2[0:SEL, 6152:6216]
        sp_ = early2[0:SEL, 6216:6280]
        smean = early2[0:SEL, 6280:6288]
        soutT = early2[:, 6288:6296]
        ioT = early2[:, 6296:6304]
        gtop = early2[0:IH, 6304:6312]
        gidx = early2[0:IH, 6312:6320].bitcast(U32)
        gidf = early2[0:IH, 6320:6328]
        idxp = early2[0:SEL, 6328:6329]
        snm = early2[0:SEL, 6329:6330]
        ssum = early2[0:SEL, 6330:6331]
        srs = early2[0:SEL, 6331:6332]
        sprob = early2[0:SEL, 6336:6400]

        S = [ctx.enter_context(nc.psum_tensor(f"S{i}", [P, 2 * BANK], F32)) for i in range(2)]
        TB = [ctx.enter_context(nc.psum_tensor(f"TB{i}", [P, BANK], F32)) for i in range(2)]
        M = ctx.enter_context(nc.psum_tensor("M", [P, BANK], F32))
        C = ctx.enter_context(nc.psum_tensor("C", [P, BANK], F32))
        YB = [S[i // 2][:, (i % 2) * BANK:(i % 2 + 1) * BANK] for i in range(4)]

        x_in = [sem(f"x_in{i}") for i in range(4)]
        wexp_in = [sem(f"wexp_in{i}") for i in range(CHUNKS)]
        wexp_again = [sem(f"wexp_again{i}") for i in range(CHUNKS)]
        whi_ready, wlo_ready, xhi_ready, xlo_ready = sem("whi_ready"), [sem(f"wlo_ready{c}") for c in range(CHUNKS)], \
            sem("xhi_ready"), sem("xlo_ready")
        masked = sem("masked")
        gate_in, latent_in, absorb_in, rope_in = sem("gate_in"), sem("latent_in"), sem("absorb_in"), sem("rope_in")
        wo_in, index_in = sem("wo_in"), sem("index_in")
        ident_made, masks_made, iotas_made = sem("ident_made"), sem("masks_made"), sem("iotas_made")
        pool_step = sem("pool_step")
        dve_step = sem("dve_step")
        var_ready, sd_ready, xn_ready = sem("var_ready"), sem("sd_ready"), sem("xn_ready")
        gap_ready, egap_ready, wts_ready = sem("gap_ready"), sem("egap_ready"), sem("wts_ready")
        y_full, y_free = [sem(f"y_full{i}") for i in range(4)], [sem(f"y_free{i}") for i in range(4)]
        t_full, t_free = [sem(f"t_full{i}") for i in range(2)], [sem(f"t_free{i}") for i in range(2)]
        m_full, m_free, c_full, c_free = sem("m_full"), sem("m_free"), sem("c_full"), sem("c_free")
        index_listed, index_spread, hot_ready = sem("index_listed"), sem("index_spread"), sem("hot_ready")
        sscore_ready, sexp_ready, sprob_ready = sem("sscore_ready"), sem("sexp_ready"), sem("sprob_ready")
        wosum_ready = sem("wosum_ready")
        khi_ready, klo_ready, qhi_ready, qlo_ready = sem("khi_ready"), sem("klo_ready"), sem("qhi_ready"), sem("qlo_ready")
        ehi_ready, elo_ready = sem("ehi_ready"), sem("elo_ready")
        cphi_ready, wshi_ready, wslo_ready, roped = sem("cphi_ready"), sem("wshi_ready"), sem("wslo_ready"), sem("roped")
        scores_ready, negmax_ready, probs_ready = sem("scores_ready"), sem("negmax_ready"), sem("probs_ready")
        rsum_ready, rwide_ready = sem("rsum_ready"), sem("rwide_ready")
        out_done = sem("out_done")

        yr = Ring(YB, y_full, y_free, Y_ORDER)
        tr = Ring([TB[0], TB[1]], t_full, t_free, T_ORDER)
        mr = Ring([M], [m_full], [m_free], M_ORDER)
        cr = Ring([C], [c_full], [c_free], C_ORDER)
        y_base = len(Y_ORDER) // 4
        tail = turn_tail()

        def y_use(key):
            if key in yr.at:
                return yr.use(key)
            i = Y_TAIL.index(key)
            return YB[i % 4], y_full[i % 4], y_free[i % 4], y_base + i // 4

        def t_use(key):
            if key in tr.at:
                return tr.use(key)
            b, prior = tail[key]
            return TB[b], t_full[b], t_free[b], prior

        def m_use(key):
            if key in mr.at:
                return mr.use(key)
            return M, m_full, m_free, mr.n + (PAIRS - 1) * 4 + 2 + key[2]

        def c_use(key):
            if key in cr.at:
                return cr.use(key)
            return C, c_full, c_free, cr.n + 2 * PAIRS + key[2]

        def rotation(g, i):
            return 4 + g * 4 + i

        def queries_at(u, g):
            if u in Q_OWN:
                return Q_OWN[u], Q_OWN[u], 1
            if u in Q_NEXT and not (isinstance(g, int) and g == PAIRS - 1):
                return 2 + Q_NEXT[u], Q_NEXT[u], 0
            return None

        def m_prior(n):
            return n - 2 + 2

        def c_group(g, group):
            return cr.n + 2 * g + group

        def probsT_drain(drain, use, v, c):
            qt, h = v // 2, v % 2
            n = min(GT, tiles_of(v) - GT * c)
            pT = pT0 if qt < GT else pT1
            drain(use, pT[:, h, GT * c:GT * c + n, P * (qt % GT):P * (qt % GT + 1)],
                  lambda b: b[:, 0:n * P].rearrange("p (k n) -> p k n", k=n))

        def low_weights(engine, f, c, loaded):
            engine.wait_ge(loaded[c], 16)
            engine.wait_ge(whi_ready, CHUNKS * f + c + 1)
            engine.tensor_tensor(wlo[f][:, c, :, :], wraw[:, c, :, :], whi[:, c, :, :].bitcast(F32), ALU.subtract) \
                .then_inc(wlo_ready[c], 1)

        def hi_scratch(half):
            return qT[QB:P, half, BANK:T].bitcast(F32R)

        wq_cols = wq.rearrange("p k h n -> p k (h n)")

        block = ctx.enter_context(nc.Block())

        @block.sync
        def _(sp):
            x_v = a["x"].rearrange("(t p) n -> p t n", p=P)
            for i in range(4):
                sp.dma_start(x[:, 2 * i:2 * i + 2, :], x_v[:, 2 * i:2 * i + 2, :]).then_inc(x_in[i], 16)
            sp.dma_start(wgate[:, :, :], a["gate_w"]).then_inc(gate_in, 16)
            sp.dma_start(bexp[:, :], a["expert_b"]).then_inc(gate_in, 16)
            for c in range(CHUNKS):
                sp.dma_start(wraw[:, c, :, :], a["expert_w"][:, c, :, :]).then_inc(wexp_in[c], 16)
            sp.dma_start(wqcT, a["W_qc"]).then_inc(absorb_in, 16)
            sp.dma_start(wkcT, a["W_kc"]).then_inc(absorb_in, 16)
            sp.dma_start(wvT, a["W_v"]).then_inc(wo_in, 16)
            sp.dma_start(wo, a["W_o"]).then_inc(wo_in, 16)
            for c in range(CHUNKS):
                sp.wait_ge(wlo_ready[c], 1)
            sp.dma_start(wq[:, :, :, KV:P], a["W_qr"]).then_inc(latent_in, 16)
            sp.dma_start(wcp[:, :, :], a["W_cp"]).then_inc(latent_in, 16)
            sp.dma_start(wkv[:, :, 0:KV], a["W_c"]).then_inc(latent_in, 16)
            sp.dma_start(wkv[:, :, KV:P], a["W_kr"]).then_inc(latent_in, 16)
            sp.dma_start(cosT, a["cos"]).then_inc(rope_in, 16)
            sp.dma_start(sinT, a["sin"]).then_inc(rope_in, 16)
            use = y_use(("y", 0, NT - 1, CHUNKS - 1))
            sp.wait_ge(use[1], use[3] + 1)
            sp.dma_start(widx, a["W_idx"]).then_inc(index_in, 16)
            sp.dma_start(widx_gate[:, :, :], a["W_gate"]).then_inc(index_in, 16)
            for n, name in enumerate(("W_sq", "W_sk", "W_sv", "W_iout")):
                sp.dma_start(ws3[:, n, :], a[name]).then_inc(index_in, 16)
            sp.wait_ge(index_listed, 1)
            sp.dma_start(idxp, gidf).then_inc(index_spread, 16)
            sp.wait_ge(wslo_ready, PAIRS)
            for c in range(CHUNKS):
                sp.dma_start(wraw[:, c, :, :], a["expert_w"][:, c, :, :]).then_inc(wexp_again[c], 16)
            out_v = out.rearrange("(t p) n -> p t n", p=P)
            for i in range(4):
                use = c_use(("bias", 1, i))
                sp.wait_ge(use[2], use[3] + 1)
                n = 2 if i < 3 else 1
                sp.dma_start(out_v[:, 2 * i:2 * i + n, :], x[:, 2 * i:2 * i + n, :]).then_inc(out_done, 16)
            use = y_use(("y", 1, NT - 1, CHUNKS - 1))
            sp.wait_ge(use[2], use[3] + 1)
            sp.dma_start(out_v[:, NT - 1:NT, :], x[:, NT - 1:NT, :]).then_inc(out_done, 16)
            sp.wait_ge(out_done, 16 * 5)

        @block.gpsimd
        def _(pool):
            steps = [0]

            def settle(ins):
                ins.then_inc(pool_step, 1)
                steps[0] += 1
                pool.wait_ge(pool_step, steps[0])

            settle(pool.memset(ident[:, :], 0.0))
            pool.affine_select(out=ident[:, :], in_=ident[:, :], compare_op=ALU.not_equal, fill=1.0, base=0,
                               pattern=[[-1, P]], channel_multiplier=1).then_inc(ident_made, 1)
            pool.iota(iota8[:, :, :], [[0, NT], [1, E]], base=0, channel_multiplier=0,
                      allow_small_or_imprecise_dtypes=True).then_inc(iotas_made, 1)
            def low_activations(f, i):
                pool.wait_ge(xhi_ready, 4 * f + i + 1)
                cols = slice(256 * i, 256 * i + 256)
                pool.tensor_tensor(xlo[:, :, cols], xraw[:, :, cols], xhi[:, :, cols].bitcast(F32), ALU.subtract) \
                    .then_inc(xlo_ready, 1)

            low_activations(0, 0)
            low_weights(pool, 0, 1, wexp_in)
            low_weights(pool, 0, 3, wexp_in)
            low_activations(0, 1)
            low_activations(0, 2)
            low_activations(0, 3)
            pool.wait_ge(ident_made, 1)
            pool.tensor_copy(identb[:, :], ident[:, :]).then_inc(masks_made, 1)
            settle(pool.memset(causal[:, :], 0.0))
            pool.affine_select(out=causal[:, :], in_=causal[:, :], compare_op=ALU.is_ge, fill=MASKED, base=0,
                               pattern=[[-1, P]], channel_multiplier=1).then_inc(masks_made, 1)
            pool.memset(ones[:, :], 1.0).then_inc(masks_made, 1)
            use = y_use(("y", 0, NT - 1, CHUNKS - 1))
            pool.wait_ge(use[1], use[3] + 1)
            pool.iota(iotaT, [[1, T]], base=0, channel_multiplier=0,
                      allow_small_or_imprecise_dtypes=True).then_inc(iotas_made, 1)
            settle(pool.memset(blockmask, 0.0))
            bm = blockmask.rearrange("p (h j) -> p h j", h=IH)
            settle(pool.affine_select(out=bm, in_=bm, compare_op=ALU.is_ge, fill=MASKED, base=0,
                                      pattern=[[-TOPK, IH], [0, TOPK]], channel_multiplier=1))
            pool.affine_select(out=bm, in_=bm, compare_op=ALU.is_ge, fill=MASKED, base=TOPK - 1,
                               pattern=[[TOPK, IH], [0, TOPK]], channel_multiplier=-1).then_inc(masks_made, 1)
            settle(pool.memset(groups, 1.0 / TOPK))
            settle(pool.affine_select(out=groups, in_=groups, compare_op=ALU.is_ge, fill=0.0, base=0,
                                      pattern=[[-TOPK, IH]], channel_multiplier=1))
            pool.affine_select(out=groups, in_=groups, compare_op=ALU.is_ge, fill=0.0, base=TOPK - 1,
                               pattern=[[TOPK, IH]], channel_multiplier=-1).then_inc(masks_made, 1)
            pool.wait_ge(wo_in, 32)
            wo_p = wo.rearrange("p (i two) n -> p i two n", two=2)
            pool.tensor_tensor(wosum, wo_p[:, :, 0, :], wo_p[:, :, 1, :], ALU.add).then_inc(wosum_ready, 1)
            pool.wait_ge(wosum_ready, 1)

            def rotate(dst, half, n, slot):
                cols = slice(BANK * half, BANK * (half + 1))
                parts = swapped[KV:P, slot, :]
                pool.tensor_tensor(turned, dst, cosT[:, cols], ALU.mult).then_inc(pool_step, 1)
                pool.tensor_tensor(parts, parts, sinT[:, cols], ALU.mult).then_inc(pool_step, 1)
                pool.wait_ge(pool_step, step_base + 2 + 2 * n)
                pool.tensor_tensor(dst, turned, parts, ALU.add).then_inc(roped, 1)
                pool.wait_ge(roped, n + 1)

            step_base = steps[0]
            def low_query_weights(pair):
                pool.wait_ge(wshi_ready, pair + 1)
                pool.tensor_tensor(ws_lo[:, :, :], wq_cols[:, :, bass.ds(pair * 2 * P, 2 * P)], ws_hi[:, :, :].bitcast(F32),
                                   ALU.subtract).then_inc(wslo_ready, 1)
                pool.wait_ge(wslo_ready, pair + 1)

            low_query_weights(0)
            pool.wait_ge(rope_in, 32)
            for i in range(2):
                use = yr.use(("latent_kv", i))
                pool.wait_ge(use[2], use[3] + 1)
                rotate(keysT[KV:P, BANK * i:BANK * (i + 1)], i, i, i)

            def query_rotate(n, h, half):
                pool.wait_ge(m_free, m_prior(n) + 1)
                rotate(qT[KV:P, h, BANK * half:BANK * (half + 1)], half, n, h)

            def spread(n, group):
                pool.wait_ge(rsum_ready, n + 1)
                wide = rsum[:, group, :, :].unsqueeze(3).to_broadcast([P, GT, 2, 64])
                one = ones[:, 0:1].unsqueeze(2).unsqueeze(3).to_broadcast([P, GT, 2, 64])
                pool.tensor_tensor(rwide[:, :, :, :], wide, one, ALU.mult).then_inc(rwide_ready, 1)
                pool.wait_ge(rwide_ready, n + 1)

            for h in range(2):
                query_rotate(2 + h, h, 0)

            def edge_low(pair):
                pool.wait_ge(ehi_ready, pair + 1)
                pool.tensor_tensor(e_lo[:, :, :], qT[:, :, BANK - P:BANK], e_hi[:, :, :].bitcast(F32), ALU.subtract) \
                    .then_inc(elo_ready, 1)
                pool.wait_ge(elo_ready, pair + 1)

            edge_low(0)

            def body(g):
                last = isinstance(g, int) and g == PAIRS - 1
                first = isinstance(g, int) and g == 0
                for u in range(UNITS):
                    if u == 1 and not first:
                        spread(2 * g - 1, 1)
                    if u == 9:
                        spread(2 * g, 0)
                    if queries_at(u, g):
                        i, h, half = queries_at(u, g)
                        query_rotate(rotation(g, i), h, half)
                    if u in LO_AT:
                        h = LO_AT[u]
                        pool.wait_ge(qhi_ready, 2 * g + h + 1)
                        pool.tensor_tensor(q_lo[:, h, :], qT[:, h, BANK:T], q_hi[:, h, :].bitcast(F32), ALU.subtract) \
                            .then_inc(qlo_ready, 1)
                        pool.wait_ge(qlo_ready, 2 * g + h + 1)
                    if u == SPLIT_AT and not last:
                        low_query_weights(g + 1)
                    if u == EDGE_AT and not last:
                        edge_low(g + 1)

            body(0)
            with pool.Fori(1, PAIRS - 1) as g:
                body(g)
            body(PAIRS - 1)
            spread(2 * PAIRS - 1, 1)
            pool.wait_ge(c_full, c_group(PAIRS - 1, 0) + 1)
            for c in range(CHUNKS):
                low_weights(pool, 1, c, wexp_again)
            for i in range(4):
                low_activations(1, i)

        @block.scalar
        def _(act):
            def root(n, half):
                act.wait_ge(var_ready, 2 * n + half + 1)
                act.activation(sd[:, 4 * half:4 * half + 4], varE[:, 4 * half:4 * half + 4], ACT.Sqrt) \
                    .then_inc(sd_ready, 1)

            def drain(use, dst, src_of, scale=None):
                bank, full, free, prior = use
                act.wait_ge(full, prior + 1)
                if scale is None:
                    act.copy(dst, src_of(bank)).then_inc(free, 1)
                else:
                    act.activation(dst, src_of(bank), ACT.Copy, scale=scale).then_inc(free, 1)

            def xnT_drain(n, i):
                drain(t_use(("xnT", n, i)), xnT[:, :, 256 * i:256 * i + 256],
                      lambda b: b[:, :].rearrange("p (k n) -> p k n", k=KD))

            def split_drain(f, n, i):
                bank, full, free, prior = t_use(("xnT", n, i))
                view = bank[:, :].rearrange("p (k n) -> p k n", k=KD)
                act.wait_ge(full, prior + 1)
                cols = slice(256 * i, 256 * i + 256)
                act.copy(xraw[:, :, cols], view).then_inc(free, 1)
                act.wait_ge(free, prior + 1)
                act.copy(xhi[:, :, cols], xraw[:, :, cols]).then_inc(xhi_ready, 1)

            def high_weights(c, loaded):
                act.wait_ge(loaded[c], 16)
                act.copy(whi[:, c, :, :], wraw[:, c, :, :]).then_inc(whi_ready, 1)

            def ffn(f, n):
                for half in range(2):
                    for i in range(2):
                        split_drain(f, n, 2 * half + i)
                    if f == 0 and half == 0:
                        high_weights(1, wexp_in)
                        root(0, 1)
                        for c in range(2, CHUNKS):
                            high_weights(c, wexp_in)
                    act.wait_ge(gap_ready, 2 * f + half + 1)
                    act.activation(egap[:, 4 * half:4 * half + 4], gap[:, 4 * half:4 * half + 4], ACT.Exp) \
                        .then_inc(egap_ready, 1)
                    if f == 1 and half == 0:
                        root(2, 1)
                    drain(t_use(("wT", f, half)), wT[:, BANK * half:BANK * (half + 1)], lambda b: b[0:E, :])

            root(0, 0)
            high_weights(0, wexp_in)
            ffn(0, 0)
            root(1, 0)

            def gate_drain(half):
                drain(yr.use(("index_gate", half)), gT[:, BANK * half:BANK * (half + 1)], lambda b: b[0:IH, :])

            def high_query_weights(pair):
                act.copy(ws_hi[:, :, :], wq_cols[:, :, bass.ds(pair * 2 * P, 2 * P)]).then_inc(wshi_ready, 1)

            for i in range(2):
                xnT_drain(1, i)
            for i in range(4):
                k, half = i // 2, i % 2
                drain(yr.use(("absorb_k", i)), wq[:, k, 8 * half:8 * half + 8, 0:KV],
                      lambda b: b[:, :].rearrange("p (h n) -> p h n", h=8))
            for i in range(4):
                use = yr.use(("absorb_k", i))
                act.wait_ge(use[2], use[3] + 1)
            act.wait_ge(latent_in, 16 * 4)
            high_query_weights(0)
            gate_drain(0)
            root(1, 1)
            for i in range(4):
                drain(yr.use(("absorb_v", i)), absV[:, 2 * i:2 * i + 2, :],
                      lambda b: b[:, :].rearrange("p (h n) -> p h n", h=2))
            for i in range(2, 4):
                xnT_drain(1, i)

            def copy_swapped(use, dst, n, slot, scale=1.0):
                bank, full, free, prior = use
                act.wait_ge(full, prior + 1)
                act.activation(dst, bank[:, :], ACT.Copy, scale=scale)
                if not isinstance(n, int) or n > 1:
                    act.wait_ge(roped, n - 1)
                h = KV + DR // 2
                act.activation(swapped[h:P, slot, :], bank[KV:h, :], ACT.Copy, scale=scale)
                act.activation(swapped[KV:h, slot, :], bank[h:P, :], ACT.Copy, scale=scale).then_inc(free, 1)

            for half in range(2):
                if half == 1:
                    gate_drain(1)
                copy_swapped(yr.use(("latent_kv", half)), keysT[:, BANK * half:BANK * (half + 1)], half, half, SCALE)
            for half in range(2):
                for m in range(2):
                    bank, full, free, prior = yr.use(("latent_q", m, half))
                    act.wait_ge(full, prior + 1)
                    cols = slice(BANK * half, BANK * (half + 1))
                    if m == 0:
                        act.copy(cp_hi[:, cols], bank[:, :]).then_inc(cphi_ready, 1)
                    else:
                        act.copy(cp_b[0:QB, cols], bank[0:QB, :])
                        act.copy(hi_scratch(half), bank[QB:P, :]).then_inc(cphi_ready, 1)

            def query_copy(n, h, half):
                copy_swapped((M, m_full, m_free, m_prior(n)), qT[:, h, BANK * half:BANK * (half + 1)], n, h)

            query_copy(2, 0, 0)
            drain(t_use(("values",)), values[:, :, :], lambda b: b[:, :].rearrange("p (t n) -> p t n", t=NT),
                  scale=1.0 / SCALE)
            query_copy(3, 1, 0)
            act.copy(k_hi[:, :], keysT[:, :]).then_inc(khi_ready, 1)

            def edge_high(pair, n):
                act.wait_ge(roped, n + 2)
                act.copy(e_hi[:, :, :], qT[:, :, BANK - P:BANK]).then_inc(ehi_ready, 1)

            edge_high(0, 2)

            def body(g):
                first = isinstance(g, int) and g == 0
                last = isinstance(g, int) and g == PAIRS - 1
                items = turn_items(g)
                for u in range(UNITS):
                    qt, h = u // 2, u % 2
                    for kind, args, b, prior in items[u]:
                        if kind == "probsT" and args[1] == 1 and u not in VECTOR_DRAINS:
                            probsT_drain(drain, (TB[b], t_full[b], t_free[b], prior), *args)
                    act.wait_ge(negmax_ready, UNITS * g + u + 1)
                    act.activation(probs[:, u % 4, 0:P * (qt + 1)], S[u % 2][:, 0:P * (qt + 1)], ACT.Exp,
                                   bias=negmax[:, u % 4:u % 4 + 1],
                                   accum_out=sums[:, qt // GT, qt % GT, h:h + 1]).then_inc(probs_ready, 1)
                    if queries_at(u, g):
                        i, head, half = queries_at(u, g)
                        query_copy(rotation(g, i), head, half)
                    if u in HI_AT:
                        h = HI_AT[u]
                        act.wait_ge(roped, rotation(g, h) + 1)
                        act.copy(q_hi[:, h, :], qT[:, h, BANK:T]).then_inc(qhi_ready, 1)
                    if u == SPLIT_AT and not last:
                        high_query_weights(g + 1)
                    if u == EDGE_AT and not last:
                        edge_high(g + 1, rotation(g, 2))
                    if first and u == INDEX_AT["sscores"]:
                        act.wait_ge(sscore_ready, 1)
                        act.activation(sp_, ssc, ACT.Exp, bias=snm, accum_out=ssum).then_inc(sexp_ready, 1)
                    for kind, args, b, prior in items[u]:
                        use = (TB[b], t_full[b], t_free[b], prior)
                        if kind == "sumsT":
                            drain(use, rT[:, args[0], :], lambda bank: bank[:, :])

            body(0)
            with act.Fori(1, PAIRS - 1) as g:
                body(g)
            body(PAIRS - 1)
            for v in range(UNITS - LAG, UNITS):
                probsT_drain(drain, t_use(("probsT", v, 1)), v, 1)
                if v >= UNITS - 2:
                    for c in range(2):
                        high_weights(2 * (v % 2) + c, wexp_again)
            drain(t_use(("sumsT", 1)), rT[:, 1, :], lambda bank: bank[:, :])
            root(2, 0)
            ffn(1, 2)

        @block.tensor
        def _(pe):
            def begin(use):
                bank, full, free, prior = use
                if not isinstance(prior, int) or prior > 0:
                    pe.wait_ge(free, prior)
                return bank

            def xnT_turn(n, half):
                for i in (2 * half, 2 * half + 1):
                    use = t_use(("xnT", n, i))
                    bank = begin(use)
                    pe.wait_ge(xn_ready, NT * n + 2 * i + 2)
                    for t in range(2):
                        for k in range(KD):
                            mm = pe.transpose(bank[:, k * 256 + t * P:k * 256 + (t + 1) * P],
                                              xn[:, 2 * i + t, k * P:(k + 1) * P], ident[:, :])
                    mm.then_inc(use[1], 1)

            def xnT_wait(n, i):
                use = t_use(("xnT", n, i))
                pe.wait_ge(use[2], use[3] + 1)

            def bias(f, i):
                use = c_use(("bias", f, i))
                bank = begin(use)
                w = t_use(("wT", f, i // 2))
                pe.wait_ge(w[2], w[3] + 1)
                for t in range(2):
                    mm = pe.matmul(bank[:, t * O:(t + 1) * O], wT[:, (2 * i + t) * P:(2 * i + t + 1) * P],
                                   bexp[:, :], start=True, stop=True)
                mm.then_inc(use[1], 1)

            def gate(f, n, half):
                use = m_use(("gate", f, half))
                bank = begin(use)
                pe.wait_ge(gate_in, 32)
                for t in range(4 * half, 4 * half + 4):
                    if t % 2 == 0:
                        xnT_wait(n, t // 2)
                    for k in range(KD):
                        mm = pe.matmul(bank[:, t * E:(t + 1) * E], xraw[:, k, t * P:(t + 1) * P], wgate[:, k, :],
                                       start=(k == 0), stop=(k == KD - 1))
                mm.then_inc(use[1], 1)

            def experts(f, t):
                for c in range(CHUNKS):
                    use = y_use(("y", f, t, c))
                    bank = begin(use)
                    if t == 0:
                        pe.wait_ge(whi_ready, CHUNKS * f + c + 1)
                        pe.wait_ge(wlo_ready[c], f + 1)
                    if t % 2 == 0 and c == 0:
                        pe.wait_ge(xhi_ready, 4 * f + t // 2 + 1)
                        pe.wait_ge(xlo_ready, 4 * f + t // 2 + 1)
                    cols = slice(t * P, (t + 1) * P)
                    for k in range(KD):
                        pe.matmul(bank, xhi[:, k, cols], whi[:, c, k, :], start=(k == 0), stop=False)
                        pe.matmul(bank, xhi[:, k, cols], wlo[f][:, c, k, :], start=False, stop=False)
                        mm = pe.matmul(bank, xlo[:, k, cols], whi[:, c, k, :], start=False, stop=(k == KD - 1))
                    mm.then_inc(use[1], 1)

            def weights_turn(f, half):
                use = t_use(("wT", f, half))
                bank = begin(use)
                pe.wait_ge(wts_ready, 2 * f + half + 1)
                for tt in range(4):
                    mm = pe.transpose(bank[0:E, tt * P:(tt + 1) * P], wts[:, 4 * half + tt, :], ident[:, :])
                mm.then_inc(use[1], 1)

            def ffn(f, n):
                experts(f, 0)
                weights_turn(f, 0)
                experts(f, 1)
                xnT_turn(n, 1)
                experts(f, 2)
                gate(f, n, 1)
                bias(f, 0)
                experts(f, 3)
                experts(f, 4)
                weights_turn(f, 1)
                bias(f, 1)
                experts(f, 5)
                bias(f, 2)
                experts(f, 6)
                bias(f, 3)
                experts(f, 7)

            pe.wait_ge(ident_made, 1)
            for _ in range(WARM_UP):
                pe.matmul(C[:, 0:P], ident[:, :], ident[:, :], start=True, stop=True)
            xnT_turn(0, 0)
            gate(0, 0, 0)
            ffn(0, 0)

            def index_gate(half):
                xnT_wait(1, 2 * half)
                xnT_wait(1, 2 * half + 1)
                use = yr.use(("index_gate", half))
                bank = begin(use)
                if half == 0:
                    pe.wait_ge(index_in, 16 * 6)
                for k in range(KD):
                    mm = pe.matmul(bank[0:IH, :], widx_gate[:, k, :], xnT[:, k, BANK * half:BANK * (half + 1)],
                                   start=(k == 0), stop=(k == KD - 1))
                mm.then_inc(use[1], 1)

            def latent_kv(half):
                xnT_wait(1, 2 * half)
                xnT_wait(1, 2 * half + 1)
                use = yr.use(("latent_kv", half))
                bank = begin(use)
                pe.wait_ge(latent_in, 16 * 4)
                for k in range(KD):
                    mm = pe.matmul(bank, wkv[:, k, :], xnT[:, k, BANK * half:BANK * (half + 1)],
                                   start=(k == 0), stop=(k == KD - 1))
                mm.then_inc(use[1], 1)

            xnT_turn(1, 0)
            pe.wait_ge(absorb_in, 32)
            for i in range(4):
                use = yr.use(("absorb_k", i))
                bank = begin(use)
                k, half = i // 2, i % 2
                for n in range(8):
                    h = 8 * half + n
                    mm = pe.matmul(bank[:, n * KV:(n + 1) * KV], wqcT[:, h, k * P:(k + 1) * P], wkcT[:, h, :],
                                   start=True, stop=True)
                mm.then_inc(use[1], 1)
            index_gate(0)
            pe.wait_ge(wo_in, 32)
            for i in range(4):
                use = yr.use(("absorb_v", i))
                bank = begin(use)
                for n in range(2):
                    for h in range(2):
                        head = 4 * i + 2 * n + h
                        mm = pe.matmul(bank[64 * h:64 * h + 64, n * O:(n + 1) * O], wvT[:, head, :], wo[:, head, :],
                                       start=True, stop=True)
                mm.then_inc(use[1], 1)

            xnT_turn(1, 1)
            latent_kv(0)
            index_gate(1)
            latent_kv(1)
            for half in range(2):
                for m in range(2):
                    use = yr.use(("latent_q", m, half))
                    bank = begin(use)
                    for k in range(KD):
                        mm = pe.matmul(bank[:, :], wcp[:, k, m * P:(m + 1) * P], xnT[:, k, BANK * half:BANK * (half + 1)],
                                       start=(k == 0), stop=(k == KD - 1))
                    mm.then_inc(use[1], 1)
            def turn_values():
                use = t_use(("values",))
                bank = begin(use)
                for i in range(2):
                    kv = yr.use(("latent_kv", i))
                    pe.wait_ge(kv[2], kv[3] + 1)
                for t in range(NT):
                    mm = pe.transpose(bank[:, t * KV:(t + 1) * KV], keysT[0:KV, t * P:(t + 1) * P], ident[0:KV, 0:KV])
                mm.then_inc(use[1], 1)

            def index_step(name):
                use = cr.use((name,))
                return use, begin(use)

            def sel_onehot():
                use, bank = index_step("onehot")
                pe.wait_ge(hot_ready, 1)
                for t in range(NT):
                    mm = pe.transpose(bank[:, t * SEL:(t + 1) * SEL], hotT[:, t * P:(t + 1) * P], ident[0:SEL, 0:SEL])
                mm.then_inc(use[1], 1)

            def sel_rows(k):
                use, bank = index_step("rows")
                for t in range(NT):
                    mm = pe.matmul(bank[:, k * SEL:(k + 1) * SEL], xn[:, t, k * P:(k + 1) * P], onehot[:, t, :],
                                   start=(t == 0), stop=(t == NT - 1))
                if k == KD - 1:
                    mm.then_inc(use[1], 1)

            def sel_states():
                use, bank = index_step("selected")
                for h in range(IH):
                    for k in range(KD):
                        mm = pe.matmul(bank[:, h * TOPK:(h + 1) * TOPK], widx[:, k, h * ID:(h + 1) * ID],
                                       rowsT[:, k, h * TOPK:(h + 1) * TOPK], start=(k == 0), stop=(k == KD - 1))
                mm.then_inc(use[1], 1)

            def sel_qkv():
                use, bank = index_step("sqkv")
                for w in range(2):
                    pe.matmul(bank[:, w * SEL:(w + 1) * SEL], ws3[:, w, :], selT, start=True, stop=True)
                pe.matmul(bank[0:SEL, P:2 * P], selT, ws3[:, 2, :], start=True, stop=True).then_inc(use[1], 1)

            def sel_scores():
                use, bank = index_step("sscores")
                pe.matmul(bank[0:SEL, 0:SEL], sqkT[:, 0, :], sqkT[:, 1, :], start=True, stop=True).then_inc(use[1], 1)

            def sel_mean():
                use, bank = index_step("smean")
                pe.wait_ge(sprob_ready, 1)
                pe.wait_ge(masks_made, 5)
                pe.matmul(bank[0:SEL, 0:IH], sprob, groups, start=True, stop=True).then_inc(use[1], 1)

            def sel_out():
                use, bank = index_step("sout")
                pe.matmul(bank[:, 0:IH], sv, smean, start=True, stop=True).then_inc(use[1], 1)

            def sel_io():
                use, bank = index_step("io")
                pe.matmul(bank[:, 0:IH], ws3[:, 3, :], soutT, start=True, stop=True).then_inc(use[1], 1)

            def sel_row():
                use, bank = index_step("io_row")
                pe.wait_ge(wosum_ready, 1)
                for h in range(IH):
                    mm = pe.matmul(bank[0:1, 0:O], ioT[:, h:h + 1], wosum[:, h, :], start=(h == 0), stop=(h == IH - 1))
                mm.then_inc(use[1], 1)

            def sel_all():
                use, bank = index_step("io_all")
                pe.matmul(bank[:, 0:O], ones[0:1, :], iorow[:, :], start=True, stop=True).then_inc(use[1], 1)

            def query(n, h, half):
                pe.wait_ge(m_free, m_prior(n))
                cols = slice(BANK * half, BANK * (half + 1))
                heads = slice(P * h, P * (h + 1))
                pe.matmul(M[:, :], ws_hi[:, 0, heads], cp_hi[:, cols], start=True, stop=False)
                pe.matmul(M[:, :], ws_hi[:, 0, heads], cp_lo[:, cols], start=False, stop=False)
                pe.matmul(M[:, :], ws_lo[:, 0, heads], cp_hi[:, cols], start=False, stop=False)
                pe.matmul(M[:, :], ws_hi[:, 1, heads], cp_b[:, cols], start=False, stop=False)
                mm = pe.matmul(M[:, :], ws_lo[:, 1, heads], cp_b[:, cols], start=False, stop=True)
                mm.then_inc(m_full, 1)

            def query_latent_wait(half):
                for m in range(2):
                    use = yr.use(("latent_q", m, half))
                    pe.wait_ge(use[2], use[3] + 1)

            sel_onehot()
            query_latent_wait(0)
            pe.wait_ge(wslo_ready, 1)
            query(2, 0, 0)
            turn_values()
            sel_rows(0)
            query(3, 1, 0)
            sel_rows(1)
            query_latent_wait(1)
            index_steps = {"selected": sel_states, "sqkv": sel_qkv, "sscores": sel_scores, "smean": sel_mean,
                           "sout": sel_out, "io": sel_io, "io_row": sel_row, "io_all": sel_all}

            def scores(g, u):
                qt, h = u // 2, u % 2
                w = P * (qt + 1)
                s = S[u % 2]
                for c in range(0, w, BANK):
                    n = min(BANK, w - c)
                    if n == BANK:
                        if qt >= GT:
                            hi, lo = [q[:, h, P * (qt - GT):P * (qt - GT + 1)] for q in (q_hi, q_lo)]
                        else:
                            hi, lo = e_hi[:, h, :], e_lo[:, h, :]
                        pe.matmul(s[:, c:c + n], hi, k_hi[:, c:c + n], start=True, stop=False)
                        pe.matmul(s[:, c:c + n], hi, k_lo[:, c:c + n], start=False, stop=False)
                        mm = pe.matmul(s[:, c:c + n], lo, k_hi[:, c:c + n], start=False, stop=True)
                        continue
                    mm = pe.matmul(s[:, c:c + n], qT[:, h, P * qt:P * (qt + 1)], keysT[:, c:c + n],
                                   start=True,
                                   stop=(u >= MASK_ON_DVE or c + n < w))
                if u >= MASK_ON_DVE:
                    mm.then_inc(scores_ready, 1)
                    return
                pe.matmul(s[:, P * qt:w], identb[:, :], causal[:, :], start=False, stop=True) \
                    .then_inc(scores_ready, 1)

            def probs_turn(use, v, c):
                bank = begin(use)
                n = min(GT, tiles_of(v) - GT * c)
                for k in range(n):
                    kt = GT * c + k
                    mm = pe.transpose(bank[:, k * P:(k + 1) * P], probs[:, v % 4, kt * P:(kt + 1) * P], ident[:, :])
                mm.then_inc(use[1], 1)

            def sums_turn(use, n):
                bank = begin(use)
                pe.wait_ge(rwide_ready, n + 1)
                for t in range(GT):
                    mm = pe.transpose(bank[:, t * P:(t + 1) * P], rwide[:, t, :, :].rearrange("p h n -> p (h n)"), ident[:, :])
                mm.then_inc(use[1], 1)

            def pv(group, kt, prior):
                if kt == 0:
                    pe.wait_ge(c_free, prior)
                pT, kts = (pT0, GT) if group == 0 else (pT1, NT)
                q0 = max(0, kt - GT * group) * P
                for h in range(2):
                    mm = pe.matmul(C[64 * h:64 * h + 64, q0:BANK], values[:, kt, :], pT[:, h, kt, q0:BANK],
                                   start=(kt == 0), stop=(kt == kts - 1))
                if kt == kts - 1:
                    mm.then_inc(c_full, 1)

            for i in range(4):
                pe.wait_ge(y_free[i], y_base)
            pe.wait_ge(tr.use(("values",))[2], tr.use(("values",))[3] + 1)
            use = cr.use(("rows",))
            pe.wait_ge(use[2], use[3] + 1)
            pe.wait_ge(masks_made, 5)

            def turn(g, kind, args, b, prior):
                use = (TB[b], t_full[b], t_free[b], prior)
                if kind == "probsT":
                    probs_turn(use, *args)
                else:
                    sums_turn(use, 2 * g - 1 if args[0] == 1 else 2 * g)

            def body(g):
                first, last = isinstance(g, int) and g == 0, isinstance(g, int) and g == PAIRS - 1
                items = turn_items(g)
                for u in range(UNITS):
                    if not first or u >= 2:
                        pe.wait_ge(probs_ready, UNITS * g + u - 1)
                    probs_items = [it for it in items[u] if it[0] == "probsT"]
                    for item in probs_items[:1]:
                        turn(g, *item)
                    if u in (0, 1, 8, 9):
                        pe.wait_ge(roped, rotation(g, {0: -2, 1: -1, 8: 0, 9: 1}[u]) + 1)
                    if u == 2 * GT - 2:
                        pe.wait_ge(klo_ready, 1)
                        pe.wait_ge(elo_ready, g + 1)
                    if u in (8, 9):
                        pe.wait_ge(qlo_ready, 2 * g + u - 8 + 1)
                    scores(g, u)
                    if not first:
                        for kt in PV_AT[1].get(u, ()):
                            pv(1, kt, c_group(g - 1, 1))
                    for kt in PV_AT[0].get(u, ()):
                        pv(0, kt, c_group(g, 0))
                    for item in probs_items[1:]:
                        turn(g, *item)
                    if queries_at(u, g):
                        i, h, half = queries_at(u, g)
                        if i == 2:
                            pe.wait_ge(wslo_ready, g + 2)
                        query(rotation(g, i), h, half)
                    if first:
                        for name, at in INDEX_AT.items():
                            if at == u:
                                index_steps[name]()
                    for item in items[u]:
                        if item[0] != "probsT":
                            turn(g, *item)

            body(0)
            with pe.Fori(1, PAIRS - 1) as g:
                body(g)
            body(PAIRS - 1)

            def project(t):
                use = y_use(("project", t))
                bank = begin(use)
                for g in range(PAIRS):
                    mm = pe.matmul(bank[:, 0:O], ctxT[:, g, t * P:(t + 1) * P], absV[:, g, :],
                                   start=(g == 0), stop=(g == PAIRS - 1))
                mm.then_inc(use[1], 1)

            for v in range(UNITS - LAG, UNITS):
                pe.wait_ge(probs_ready, UNITS * (PAIRS - 1) + v + 1)
                for c in range(chunks_of(v)):
                    probs_turn(t_use(("probsT", v, c)), v, c)
                if v == UNITS - 2:
                    pe.wait_ge(c_free, c_group(PAIRS - 1, 0) + 1)
                if v >= UNITS - 2:
                    for t in range(2):
                        project(2 * (v % 2) + t)
            sums_turn(t_use(("sumsT", 1)), 2 * PAIRS - 1)
            for c in range(2):
                use = t_use(("probsT", UNITS - 1, c))
                pe.wait_ge(use[2], use[3] + 1)
            for kt in range(NT):
                pv(1, kt, c_group(PAIRS - 1, 1))
            xnT_turn(2, 0)
            pe.wait_ge(c_free, c_group(PAIRS - 1, 1) + 1)
            for t in range(GT, NT):
                project(t)
            gate(1, 2, 0)
            ffn(1, 2)

        @block.vector
        def _(dve):
            steps = [0]

            def settle(ins):
                ins.then_inc(dve_step, 1)
                steps[0] += 1
                dve.wait_ge(dve_step, steps[0])

            def tick(ins):
                ins.then_inc(dve_step, 1)
                steps[0] += 1

            def norm_stats(n, half):
                ts = range(4 * half, 4 * half + 4)
                hs = slice(4 * half, 4 * half + 4)
                for t in ts:
                    if n == 0 and t % 2 == 0:
                        dve.wait_ge(x_in[t // 2], 16)
                    tick(dve.bn_stats(stats[:, t, :], x[:, t, :]))
                dve.wait_ge(dve_step, steps[0])
                for t in ts:
                    tick(dve.bn_aggr(mv[:, t, :], stats[:, t, :]))
                dve.wait_ge(dve_step, steps[0])
                dve.tensor_scalar(varE[:, hs], mv[:, hs, 1], EPS, None, ALU.add).then_inc(var_ready, 1)

            def norm_apply(n, half):
                hs = slice(4 * half, 4 * half + 4)
                dve.wait_ge(sd_ready, 2 * n + half + 1)
                settle(dve.reciprocal(rs0[:, hs], sd[:, hs]))
                settle(dve.scalar_tensor_tensor(out=rs0[:, hs], in0=varE[:, hs], scalar=0.5, in1=rs0[:, hs],
                                                op0=ALU.mult, op1=ALU.mult))
                settle(dve.scalar_tensor_tensor(out=rs0[:, hs], in0=sd[:, hs], scalar=0.5, in1=rs0[:, hs],
                                                op0=ALU.mult, op1=ALU.add))
                settle(dve.reciprocal(rstd[:, hs], rs0[:, hs]))
                for t in range(4 * half, 4 * half + 4):
                    dve.tensor_scalar(xn[:, t, :], x[:, t, :], mv[:, t, 0:1], rstd[:, t:t + 1],
                                      ALU.subtract, ALU.mult).then_inc(xn_ready, 1)

            def route(f, half):
                ts = range(4 * half, 4 * half + 4)
                hs = slice(4 * half, 4 * half + 4)
                n = 2 * f + half + 1
                bank, full, free, prior = m_use(("gate", f, half))
                dve.wait_ge(full, prior + 1)
                dve.tensor_copy(logits[:, hs, :], bank[:, 32 * half:32 * half + 32].rearrange("p (t e) -> p t e", e=E)) \
                    .then_inc(free, 1)
                dve.wait_ge(free, prior + 1)
                for t in ts:
                    tick(dve.max(top[:, t, :], logits[:, t, :]))
                dve.wait_ge(dve_step, steps[0])
                dve.tensor_tensor(gap[:, hs], top[:, hs, 1], top[:, hs, 0], ALU.subtract).then_inc(gap_ready, 1)
                for t in ts:
                    tick(dve.max_index(topi[:, t, :], top[:, t, :], logits[:, t, :]))
                dve.wait_ge(dve_step, steps[0])
                settle(dve.tensor_copy(topf[:, hs, :], topi[:, hs, 0:2]))
                if n == 1:
                    dve.wait_ge(iotas_made, 1)
                for k in range(2):
                    tick(dve.tensor_tensor(hot[:, k, hs, :], iota8[:, hs, :],
                                           topf[:, hs, k:k + 1].to_broadcast([P, 4, E]), ALU.is_equal))
                dve.wait_ge(egap_ready, n)
                settle(dve.tensor_scalar(w2[:, hs], egap[:, hs], 2.0, 2.0, ALU.mult, ALU.add))
                settle(dve.reciprocal(w1[:, hs], w2[:, hs]))
                settle(dve.tensor_tensor(w2[:, hs], w1[:, hs], egap[:, hs], ALU.mult))
                for k, w in enumerate((w1, w2)):
                    tick(dve.tensor_tensor(hot[:, k, hs, :], hot[:, k, hs, :],
                                           w[:, hs].unsqueeze(2).to_broadcast([P, 4, E]), ALU.mult))
                dve.wait_ge(dve_step, steps[0])
                dve.tensor_tensor(wts[:, hs, :], hot[:, 0, hs, :], hot[:, 1, hs, :], ALU.add).then_inc(wts_ready, 1)
                dve.wait_ge(wts_ready, n)

            def combine(f, t):
                for c in range(CHUNKS):
                    bank, full, free, prior = y_use(("y", f, t, c))
                    dve.wait_ge(full, prior + 1)
                    for e in range(2):
                        ins = dve.scalar_tensor_tensor(out=x[:, t, :], in0=bank[:, e * O:(e + 1) * O],
                                                       scalar=wts[:, t, 2 * c + e:2 * c + e + 1], in1=x[:, t, :],
                                                       op0=ALU.mult, op1=ALU.add)
                        if e == 0:
                            settle(ins)
                        else:
                            ins.then_inc(free, 1)
                            dve.wait_ge(free, prior + 1)

            def add_bias(f, i):
                bank, full, free, prior = c_use(("bias", f, i))
                dve.wait_ge(full, prior + 1)
                ins = dve.tensor_tensor(x[:, 2 * i:2 * i + 2, :], bank[:, :].rearrange("p (t n) -> p t n", t=2),
                                        x[:, 2 * i:2 * i + 2, :], ALU.add)
                ins.then_inc(free, 1)
                dve.wait_ge(free, prior + 1)

            norm_stats(0, 0)
            norm_apply(0, 0)
            low_weights(dve, 0, 0, wexp_in)
            norm_stats(0, 1)
            norm_apply(0, 1)
            low_weights(dve, 0, 2, wexp_in)
            route(0, 0)
            for t in range(3):
                combine(0, t)
            add_bias(0, 0)
            route(0, 1)
            combine(0, 3)
            combine(0, 4)
            add_bias(0, 1)
            norm_stats(1, 0)
            combine(0, 5)
            norm_apply(1, 0)
            add_bias(0, 2)
            combine(0, 6)
            add_bias(0, 3)
            combine(0, 7)
            norm_stats(1, 1)
            norm_apply(1, 1)

            def low_query_latent(m, half):
                bank, full, free, prior = yr.use(("latent_q", m, half))
                cols = slice(BANK * half, BANK * (half + 1))
                dve.wait_ge(cphi_ready, 2 * half + m + 1)
                if m == 0:
                    ins = dve.tensor_tensor(cp_lo[:, cols], bank[:, :], cp_hi[:, cols].bitcast(F32), ALU.subtract)
                else:
                    ins = dve.tensor_tensor(cp_b[QB:P, cols], bank[QB:P, :], hi_scratch(half).bitcast(F32), ALU.subtract)
                ins.then_inc(free, 1)

            def take(name, dst, src):
                bank, full, free, prior = cr.use((name,))
                dve.wait_ge(full, prior + 1)
                dve.tensor_copy(dst, src(bank)).then_inc(free, 1)

            for i in range(2):
                use = yr.use(("index_gate", i))
                dve.wait_ge(use[2], use[3] + 1)
            settle(dve.max(gtop, gT))
            settle(dve.max_index(gidx, gtop, gT))
            dve.tensor_copy(gidf, gidx).then_inc(index_listed, 1)
            for m in range(2):
                low_query_latent(m, 0)
            dve.wait_ge(index_spread, 16)
            dve.wait_ge(iotas_made, 2)
            dve.tensor_scalar(hotT, iotaT, idxp, None, ALU.is_equal).then_inc(hot_ready, 1)
            for m in range(2):
                low_query_latent(m, 1)
            take("onehot", onehot, lambda b: b[:, :].rearrange("p (t s) -> p t s", t=NT))
            take("rows", rowsT, lambda b: b[:, 0:KD * SEL].rearrange("p (k s) -> p k s", k=KD))

            dve.wait_ge(khi_ready, 1)
            dve.tensor_tensor(k_lo[:, :], keysT[:, :], k_hi[:, :].bitcast(F32), ALU.subtract).then_inc(klo_ready, 1)

            def index_step(name):
                if name == "selected":
                    take("selected", selT, lambda b: b[:, 0:SEL])
                elif name == "sqkv":
                    bank, full, free, prior = cr.use(("sqkv",))
                    dve.wait_ge(full, prior + 1)
                    tick(dve.tensor_copy(sv, bank[0:SEL, P:2 * P]))
                    dve.tensor_copy(sqkT, bank[:, 0:2 * SEL].rearrange("p (w s) -> p w s", w=2)).then_inc(free, 1)
                elif name == "sscores":
                    bank, full, free, prior = cr.use(("sscores",))
                    dve.wait_ge(full, prior + 1)
                    dve.wait_ge(masks_made, 5)
                    dve.scalar_tensor_tensor(out=ssc, in0=bank[0:SEL, 0:SEL], scalar=1.0 / float(np.sqrt(ID)),
                                             in1=blockmask, op0=ALU.mult, op1=ALU.add).then_inc(free, 1)
                    dve.wait_ge(free, prior + 1)
                    dve.tensor_reduce(snm, ssc, AX.X, ALU.max, negate=True).then_inc(sscore_ready, 1)
                elif name == "probabilities":
                    dve.wait_ge(sexp_ready, 1)
                    settle(dve.reciprocal(srs, ssum))
                    dve.tensor_scalar(sprob, sp_, srs, None, ALU.mult).then_inc(sprob_ready, 1)
                elif name == "smean":
                    take("smean", smean, lambda b: b[0:SEL, 0:IH])
                elif name == "sout":
                    take("sout", soutT, lambda b: b[:, 0:IH])
                elif name == "io":
                    take("io", ioT, lambda b: b[:, 0:IH])
                elif name == "io_row":
                    take("io_row", iorow[:, :], lambda b: b[0:1, 0:O])
                else:
                    bank, full, free, prior = cr.use(("io_all",))
                    dve.wait_ge(full, prior + 1)
                    dve.tensor_tensor(x[:, :, :], x[:, :, :], bank[:, 0:O].unsqueeze(1).to_broadcast([P, NT, O]), ALU.add) \
                        .then_inc(free, 1)

            def drain(use, dst, src_of):
                bank, full, free, prior = use
                dve.wait_ge(full, prior + 1)
                dve.tensor_copy(dst, src_of(bank)).then_inc(free, 1)

            def group_sums(group, n):
                dve.wait_ge(probs_ready, n)
                dve.reciprocal(rsum[:, group, :, :], sums[:, group, :, :]).then_inc(rsum_ready, 1)

            def context(g, group, prior, r_use):
                dve.wait_ge(c_full, prior + 1)
                dve.wait_ge(r_use[2], r_use[3] + 1)
                flat = ctxT[:, :, :].rearrange("p g n -> p (g n)")
                dve.tensor_tensor(flat[:, bass.ds(g * T + group * BANK, BANK)], C[:, :], rT[:, group, :], ALU.mult) \
                    .then_inc(c_free, 1)

            def sums_use(items, group):
                (kind, args, b, prior), = [i for i in items[R_AT[group]] if i[0] == "sumsT"]
                return TB[b], t_full[b], t_free[b], prior

            def body(g):
                first = isinstance(g, int) and g == 0
                items = turn_items(g)
                for u in range(UNITS):
                    qt = u // 2
                    for kind, args, b, prior in items[u]:
                        if kind == "probsT" and (args[1] == 0 or u in VECTOR_DRAINS):
                            probsT_drain(drain, (TB[b], t_full[b], t_free[b], prior), *args)
                    dve.wait_ge(scores_ready, UNITS * g + u + 1)
                    if u >= MASK_ON_DVE:
                        diagonal = S[u % 2][:, P * qt:P * (qt + 1)]
                        dve.tensor_tensor(diagonal, diagonal, causal[:, :], ALU.add).then_inc(masked, 1)
                        dve.wait_ge(masked, (UNITS - MASK_ON_DVE) * g + u - MASK_ON_DVE + 1)
                    dve.tensor_reduce(negmax[:, u % 4:u % 4 + 1], S[u % 2][:, 0:P * (qt + 1)], AX.X, ALU.max,
                                      negate=True).then_inc(negmax_ready, 1)
                    if first:
                        for name, at in (*INDEX_AT.items(), ("probabilities", INDEX_AT["smean"] - 1)):
                            if at == u:
                                index_step(name)
                    if u == CONTEXT_AT[0] and not first:
                        b0 = sums_before(g)
                        context(g - 1, 0, c_group(g - 1, 0), b0)
                    if u == 1 and not first:
                        group_sums(1, UNITS * g)
                    if u == 9:
                        group_sums(0, UNITS * g + 8)
                    if u == CONTEXT_AT[1] and not first:
                        context(g - 1, 1, c_group(g - 1, 1), sums_use(items, 1))

            def sums_before(g):
                if isinstance(g, int):
                    return sums_use(turn_items(g - 1), 0)
                return sums_use(turn_items(g - 1), 0)

            body(0)
            with dve.Fori(1, PAIRS - 1) as g:
                body(g)
            body(PAIRS - 1)
            def residual(t):
                bank, full, free, prior = y_use(("project", t))
                dve.wait_ge(full, prior + 1)
                ins = dve.tensor_tensor(x[:, t, :], bank[:, 0:O], x[:, t, :], ALU.add)
                ins.then_inc(free, 1)
                dve.wait_ge(free, prior + 1)

            context(PAIRS - 1, 0, c_group(PAIRS - 1, 0), sums_before(PAIRS))
            for v in range(UNITS - LAG, UNITS - 1):
                probsT_drain(drain, t_use(("probsT", v, 0)), v, 0)
            group_sums(1, UNITS * PAIRS)
            residual(0)
            residual(1)
            probsT_drain(drain, t_use(("probsT", UNITS - 1, 0)), UNITS - 1, 0)
            residual(2)
            residual(3)
            norm_stats(2, 0)
            norm_apply(2, 0)
            last_r = t_use(("sumsT", 1))
            context(PAIRS - 1, 1, c_group(PAIRS - 1, 1), last_r)
            for t in range(GT, NT):
                residual(t)
            norm_stats(2, 1)
            route(1, 0)
            combine(1, 0)
            norm_apply(2, 1)
            combine(1, 1)
            combine(1, 2)
            add_bias(1, 0)
            route(1, 1)
            combine(1, 3)
            combine(1, 4)
            add_bias(1, 1)
            combine(1, 5)
            add_bias(1, 2)
            combine(1, 6)
            add_bias(1, 3)
            combine(1, 7)


def kernel(L0_attn_x, L0_attn_W_c, L0_attn_W_cp, L0_attn_W_qc, L0_attn_W_qr, L0_attn_W_kc, L0_attn_W_kr, L0_attn_W_v,
           L0_attn_W_o, L0_attn_W_idx, L0_attn_W_gate, L0_attn_W_sq, L0_attn_W_sk, L0_attn_W_sv, L0_attn_W_iout,
           L0_ffn_gate_w, L0_ffn_expert_w, L0_ffn_expert_b):
    import concourse.bacc as bacc
    from concourse.bass_utils import run_bass_kernel_spmd

    halves = np.concatenate([np.arange(0, DR, 2), np.arange(1, DR, 2)])
    inv = 1.0 / 10000.0 ** (np.arange(0, DR, 2)[:DR // 2].astype(np.float32) / DR)
    freqs = np.outer(np.arange(T, dtype=np.float32), inv)
    cos, sin = np.cos(freqs).astype(np.float32), np.sin(freqs).astype(np.float32)

    twice = np.concatenate([np.arange(QL), np.arange(QA, QL)])

    def np_(v):
        return np.asarray(v)

    def tiles(v, p):
        v = np_(v)
        return v.reshape(v.shape[0] // p, p, -1).transpose(1, 0, 2)

    data = {
        "x": np_(L0_attn_x).reshape(T, D),
        "gate_w": tiles(np_(L0_ffn_gate_w).T, P),
        "expert_b": np_(L0_ffn_expert_b),
        "expert_w": np_(L0_ffn_expert_w).reshape(CHUNKS, 2, O, KD, P).transpose(4, 0, 3, 1, 2).reshape(P, CHUNKS, KD, 2 * O),
        "W_qc": np_(L0_attn_W_qc)[twice].reshape(QA + 2 * QB, NH, DK).transpose(2, 1, 0),
        "W_kc": np_(L0_attn_W_kc).reshape(KV, NH, DK).transpose(2, 1, 0),
        "W_v": np_(L0_attn_W_v).reshape(KV, NH, DV).transpose(2, 1, 0),
        "W_o": np_(L0_attn_W_o).reshape(NH, DV, D).transpose(1, 0, 2),
        "W_qr": np_(L0_attn_W_qr)[twice].reshape(2, P, NH, DR)[..., halves].transpose(1, 0, 2, 3),
        "W_cp": tiles(np_(L0_attn_W_cp)[:, twice], P),
        "W_c": tiles(L0_attn_W_c, P),
        "W_kr": tiles(np_(L0_attn_W_kr)[:, halves], P),
        "cos": np.concatenate([cos, cos], axis=1).T,
        "sin": np.concatenate([-sin, sin], axis=1).T,
        "W_idx": tiles(L0_attn_W_idx, P),
        "W_gate": tiles(L0_attn_W_gate, P),
        "W_sq": np_(L0_attn_W_sq),
        "W_sk": np_(L0_attn_W_sk),
        "W_sv": np_(L0_attn_W_sv),
        "W_iout": np_(L0_attn_W_iout)[:, 0:DV],
    }
    nc = bacc.Bacc("TRN2", target_bir_lowering=False, num_devices=1)
    arrays, a = {}, {}
    for name, v in data.items():
        v = np.ascontiguousarray(v)
        arrays[f"in_{name}"] = v
        a[name] = nc.dram_tensor(f"in_{name}", v.shape, mybir.dt.from_np(v.dtype), kind="ExternalInput").ap()
    out = nc.dram_tensor("out", (T, D), F32, kind="ExternalOutput").ap()
    build(nc, a, out)
    r = run_bass_kernel_spmd(nc, [arrays], core_ids=[0])
    return r.results[0]["out"].reshape(1, T, D)
```
